# Optimizing a Trainium2 kernel written in Bass

```python
import numpy as np
import jax
import jax.numpy as jnp

def _softmax(x, axis=-1):
    return jax.nn.softmax(x, axis=axis)

def _gelu(x):
    return jax.nn.gelu(x, approximate=True)

def _silu(x):
    return jax.nn.silu(x)

def _sigmoid(x):
    return jax.nn.sigmoid(x)

def _layernorm(x, axis=-1, eps=1e-05):
    m = jnp.mean(x, axis=axis, keepdims=True)
    v = jnp.var(x, axis=axis, keepdims=True)
    return (x - m) / jnp.sqrt(v + eps)

def _scatter_add(tgt, idx, src, axis=0):
    return tgt.at[idx].add(src)

def _segment_sum(src, seg, n):
    return jax.ops.segment_sum(src, seg, n)
kernel_name = 'mk_seq_preln_d1_jaxref_r4_6d7700'

def setup_inputs(seed: int=0):
    np.random.seed(seed)
    _w = jnp.asarray

    def _L0_attn_setup():
        import jax, jax.numpy as jnp
        import numpy as np
        DIM = 256
        NUM_HEADS = 16
        NUM_KV_HEADS = 2
        HEAD_DIM = DIM // NUM_HEADS
        REPEATS = NUM_HEADS // NUM_KV_HEADS
        WINDOW = 64
        HALF = WINDOW // 2
        BATCH, SEQ = (2, 512)
        key = jax.random.key(seed)
        ks = jax.random.split(key, 9)
        sc = 1.0 / np.sqrt(DIM)
        return {'x': jax.random.normal(ks[0], (BATCH, SEQ, DIM), jnp.float32), 'Wq': jax.random.normal(ks[1], (DIM, NUM_HEADS * HEAD_DIM), jnp.float32) * sc, 'bq': jax.random.normal(ks[2], (NUM_HEADS * HEAD_DIM,), jnp.float32) * 0.01, 'Wk': jax.random.normal(ks[3], (DIM, NUM_KV_HEADS * HEAD_DIM), jnp.float32) * sc, 'bk': jax.random.normal(ks[4], (NUM_KV_HEADS * HEAD_DIM,), jnp.float32) * 0.01, 'Wv': jax.random.normal(ks[5], (DIM, NUM_KV_HEADS * HEAD_DIM), jnp.float32) * sc, 'bv': jax.random.normal(ks[6], (NUM_KV_HEADS * HEAD_DIM,), jnp.float32) * 0.01, 'Wo': jax.random.normal(ks[7], (DIM, DIM), jnp.float32) * sc, 'bo': jax.random.normal(ks[8], (DIM,), jnp.float32) * 0.01}
    _L0_attn_in = _L0_attn_setup()

    def _L0_ffn_setup():
        import jax, jax.numpy as jnp
        import numpy as np
        HIDDEN = 256
        NUM_EXPERTS = 16
        TOP_K = 6
        EPS = 1e-10
        key = jax.random.key(seed)
        k1, k2, k3, k4 = jax.random.split(key, 4)
        tokens = jax.random.normal(k1, (4, 512, HIDDEN), dtype=jnp.float32)
        bound = 1.0 / np.sqrt(HIDDEN)
        router_w = jax.random.uniform(k2, (NUM_EXPERTS, HIDDEN), jnp.float32, -bound, bound)
        router_b = jax.random.uniform(k3, (NUM_EXPERTS,), jnp.float32, -bound, bound)
        expert_w = jax.random.normal(k4, (NUM_EXPERTS, HIDDEN, HIDDEN), dtype=jnp.float32) / np.sqrt(HIDDEN)
        return {'tokens': tokens, 'router_w': router_w, 'router_b': router_b, 'expert_w': expert_w}
    _L0_ffn_in = _L0_ffn_setup()
    _d = {'L0_attn_x': _L0_attn_in['x'], 'L0_attn_Wq': _L0_attn_in['Wq'], 'L0_attn_bq': _L0_attn_in['bq'], 'L0_attn_Wk': _L0_attn_in['Wk'], 'L0_attn_bk': _L0_attn_in['bk'], 'L0_attn_Wv': _L0_attn_in['Wv'], 'L0_attn_bv': _L0_attn_in['bv'], 'L0_attn_Wo': _L0_attn_in['Wo'], 'L0_attn_bo': _L0_attn_in['bo'], 'L0_ffn_router_w': _L0_ffn_in['router_w'], 'L0_ffn_router_b': _L0_ffn_in['router_b'], 'L0_ffn_expert_w': _L0_ffn_in['expert_w']}
    _x0 = _d['L0_attn_x']
    _d['L0_attn_x'] = jax.random.normal(jax.random.fold_in(jax.random.key(seed), 1), (4, 1024, 256), dtype=_x0.dtype)
    del _x0
    return _d

def reference(L0_attn_x, L0_attn_Wq, L0_attn_bq, L0_attn_Wk, L0_attn_bk, L0_attn_Wv, L0_attn_bv, L0_attn_Wo, L0_attn_bo, L0_ffn_router_w, L0_ffn_router_b, L0_ffn_expert_w):

    def _L0_attn_ref(x, Wq, bq, Wk, bk, Wv, bv, Wo, bo):
        import jax, jax.numpy as jnp
        import numpy as np
        DIM = 256
        NUM_HEADS = 16
        NUM_KV_HEADS = 2
        HEAD_DIM = DIM // NUM_HEADS
        REPEATS = NUM_HEADS // NUM_KV_HEADS
        WINDOW = 64
        HALF = WINDOW // 2
        BATCH, SEQ = (2, 512)
        b, s, _ = x.shape
        q = (x @ Wq + bq).reshape(b, s, NUM_HEADS, HEAD_DIM).transpose(0, 2, 1, 3)
        k = (x @ Wk + bk).reshape(b, s, NUM_KV_HEADS, HEAD_DIM).transpose(0, 2, 1, 3)
        v = (x @ Wv + bv).reshape(b, s, NUM_KV_HEADS, HEAD_DIM).transpose(0, 2, 1, 3)
        kp = jnp.pad(k, ((0, 0), (0, 0), (HALF, HALF), (0, 0)))
        vp = jnp.pad(v, ((0, 0), (0, 0), (HALF, HALF), (0, 0)))
        idx = jnp.arange(s)[:, None] + jnp.arange(WINDOW)[None, :]
        k_win = kp[:, :, idx]
        v_win = vp[:, :, idx]
        qg = q.reshape(b, NUM_KV_HEADS, REPEATS, s, HEAD_DIM)
        scores = jnp.einsum('bgrsd,bgswd->bgrsw', qg, k_win)
        probs = jax.nn.softmax(scores, axis=-1)
        out = jnp.einsum('bgrsw,bgswd->bgrsd', probs, v_win)
        out = out.reshape(b, NUM_HEADS, s, HEAD_DIM).transpose(0, 2, 1, 3).reshape(b, s, DIM)
        return out @ Wo + bo

    def _L0_ffn_ref(tokens, router_w, router_b, expert_w):
        import jax, jax.numpy as jnp
        import numpy as np
        HIDDEN = 256
        NUM_EXPERTS = 16
        TOP_K = 6
        EPS = 1e-10
        B, S, H = tokens.shape
        E = expert_w.shape[0]
        T = B * S
        logits = jnp.einsum('bsh,eh->bse', tokens, router_w) + router_b
        probs = jax.nn.softmax(logits, axis=-1)
        top_p, top_i = jax.lax.top_k(probs, TOP_K)
        top_p = top_p / (jnp.sum(top_p, axis=-1, keepdims=True) + EPS)
        x = tokens.reshape(T, H)
        flat_i = top_i.reshape(T, TOP_K)
        flat_p = top_p.reshape(T, TOP_K)
        gate = jnp.zeros((T, E), dtype=flat_p.dtype)
        gate = gate.at[jnp.arange(T)[:, None], flat_i].add(flat_p)
        acc = jnp.maximum(jnp.sum(gate, axis=-1), EPS)
        out = jnp.zeros_like(x)
        for e in range(E):
            out = out + x @ expert_w[e] * gate[:, e:e + 1]
        out = (out / acc[:, None]).reshape(B, S, H)
        out = out + EPS * jnp.sum(top_p, axis=-1, keepdims=True)
        return out
    x = L0_attn_x
    x = x + _L0_attn_ref(_layernorm(x, axis=-1), L0_attn_Wq, L0_attn_bq, L0_attn_Wk, L0_attn_bk, L0_attn_Wv, L0_attn_bv, L0_attn_Wo, L0_attn_bo)
    x = x + _L0_ffn_ref(_layernorm(x, axis=-1), L0_ffn_router_w, L0_ffn_router_b, L0_ffn_expert_w)
    return x

_drawn_inputs = setup_inputs


def setup_inputs(seed=0):
    import zlib

    import numpy as np

    out = dict(_drawn_inputs(seed))
    spreads = {}
    factors = {'L0_attn_bk': 200.0, 'L0_attn_bo': 3.373, 'L0_attn_bv': 2.796, 'L0_attn_bq': 2.736}
    for name, (base, spread) in spreads.items():
        noise = np.random.default_rng([zlib.crc32(name.encode()), seed]).standard_normal(out[name].shape)
        drawn = base * np.exp(spread * noise) if base else spread * noise
        out[name] = jnp.asarray(drawn.astype(out[name].dtype))
    for name, factor in factors.items():
        out[name] = (out[name] * factor).astype(out[name].dtype)
    return out
```

```python
from contextlib import ExitStack

import concourse.bass as bass
from concourse import mybir

P = 128
DIM = 256
KC = DIM // P
HEADS = 16
GROUPS = 2
HD = DIM // HEADS
PER_GROUP = HEADS // GROUPS
WINDOW = 64
HALF = WINDOW // 2
BATCH, SEQ = 4, 1024
BLOCK = 512
HALO = BLOCK + 2 * HALF
BLOCKS = BATCH * SEQ // BLOCK
TILES = BLOCK // P
SUB = 64
SUBS = BLOCK // SUB
PAIRS = HEADS // 2
SLOTS_QK = 6
ROWS = SLOTS_QK * HD
MAXPARTS = 2
Q_PART = [0, 0, 0, 1, 1, 2]
K_PART = [0, 1, 2, 0, 1, 0]
VW = 3 * HD + 1
EXPERTS = 16
R0 = 2 * GROUPS * HD
TOP_K = 6
EPS_LN = 1e-5
EPS_GATE = 1e-10
FAR = -1e30
HUGE = 3e38
EG = EXPERTS // 2
QK_LOADS = 16 * SLOTS_QK * (GROUPS + 1)
BY_ACT = (2, 5)
BY_DVE = tuple(g for g in range(EG) if g not in BY_ACT)
STAGES = 4

ALU = mybir.AluOpType
ACT = mybir.ActivationFunctionType
AX = mybir.AxisListType
F32 = mybir.dt.float32
F32R = mybir.dt.float32r
BF16 = mybir.dt.bfloat16
F16 = mybir.dt.float16
U8 = mybir.dt.uint8

FRONT_ORDER = [("LN1", 0), ("T", 0), ("T", 1), ("T", 2), ("Q", 0), ("Q", 1), ("Qb", 0), ("Qb", 1),
               ("KV", 0), ("KV", 1), ("KVb", 0), ("VT", 0), ("VTb", 0)]
SLOTS = [
    [("S", 0), ("M",), ("MT", 0), ("M",)],
    [("S", 1), ("M",), ("MT", 1), ("M",), ("ST", 0)],
    [("S", 2), ("LN1", 0), ("M",), ("MT", 2), ("M",), ("PV", 0), ("ST", 1)],
    [("S", 3), ("M",), ("MT", 3), ("M",), ("T", 0), ("PV", 1), ("ST", 2)],
    [("S", 4), ("M",), ("MT", 4), ("M",), ("T", 1), ("PV", 2), ("ST", 3), ("M",), ("OT", 0), ("M",), ("WO", 0)],
    [("S", 5), ("M",), ("MT", 5), ("M",), ("T", 2), ("PV", 3), ("ST", 4), ("M",), ("X2T", 0)],
    [("S", 6), ("M",), ("MT", 6), ("M",), ("Q", 0), ("PV", 4), ("ST", 5), ("OT", 1), ("Qb", 0), ("M",), ("WO", 1)],
    [("S", 7), ("M",), ("MT", 7), ("M",), ("Q", 1), ("PV", 5), ("ST", 6), ("X2T", 1), ("Qb", 1)],
    [("M",), ("KV", 0), ("PV", 6), ("ST", 7), ("M",), ("OT", 2), ("M",), ("WO", 2)],
    [("M",), ("PV", 7), ("KV", 1), ("M",), ("KVb", 0), ("X2T", 2), ("M",), ("VT", 0)],
    [("M",), ("VTb", 0), ("OT", 3), ("M",), ("WO", 3)],
    [("M",), ("X2T", 3), ("M",)],
    [("LT", 0), ("M",), ("LG", 0), ("M",)],
]
ORDER, _m = [], 0
for _slot in SLOTS:
    for _tag in _slot:
        if _tag[0] == "M":
            ORDER.append(("M", _m))
            _m += 1
        else:
            ORDER.append(_tag)
assert _m == TILES * EG, _m
IN_FRONT = {t[0] for t in FRONT_ORDER}
USES = ("MT", "T", "Q", "KV", "VT", "OT", "WO", "X2T", "LT", "LG")
FRONT_USES = [t for t in FRONT_ORDER if t[0] in USES]
STEP_USES = [t for t in ORDER if t[0] in USES]
LAST_USES = [t for t in STEP_USES if t[0] not in IN_FRONT]


def nth(block, per, k):
    return block * per + k


ACC_0, SUM_0 = 2, 1


def build(nc, x_halo, wq, bq, wk, bk, wv, bv, wo, bo, rwt, rb, ew, out):
    with ExitStack() as ctx:
        def sb(name, shape, dt):
            return ctx.enter_context(nc.sbuf_tensor(name, shape, dt))

        def ps(name, shape, dt=F32):
            return ctx.enter_context(nc.psum_tensor(name, shape, dt))

        def sem(name):
            return ctx.enter_context(nc.semaphore(name))

        q_dram = nc.dram_tensor("q_parts", [BLOCKS, GROUPS, 3, SUBS, P, SUB], BF16).ap()
        k_dram = nc.dram_tensor("k_parts", [BLOCKS, 3, GROUPS * HD, HALO], BF16).ap()

        s_ps = ps("s_ps", [P, PAIRS, P])
        st_ps = ps("st_ps", [P, GROUPS, 512])
        pv_ps = ps("pv_ps", [P, 512])
        e_ps = ps("e_ps", [P, 2, 512])
        misc = ps("misc", [P, 512])

        stage = sb("stage", [P, STAGES, 512], F32)
        wq_h, wq_l = sb("wq_h", [P, KC, DIM], F32R), sb("wq_l", [P, KC, DIM], F32R)
        wkv_h, wkv_l = sb("wkv_h", [P, KC, P], F32R), sb("wkv_l", [P, KC, P], F32R)
        wo_h, wo_l = sb("wo_h", [P, 2, DIM], F32R), sb("wo_l", [P, 2, DIM], F32R)
        we_h = sb("we_h", [P, KC, EXPERTS, DIM], F32R)
        we_l = sb("we_l", [P, KC, EXPERTS, DIM], F32R)
        bq_c = sb("bq_c", [P, GROUPS], F32)
        bkv = sb("bkv", [1, 64], F32)
        bkv_h, bkv_l = sb("bkv_h", [1, P], F32R), sb("bkv_l", [1, P], F32R)
        bo_b = sb("bo_b", [P, DIM], F32)
        rb_c = sb("rb_c", [R0 + EXPERTS, 1], F32)
        valid = sb("valid", [1, HALO + HALF], F32R)
        ident = sb("ident", [P, P], F32)
        ident_b = sb("ident_b", [P, P], BF16)
        far = sb("far", [P, PER_GROUP, SUB], BF16)
        upper = sb("upper", [P, PAIRS, SUB], U8)
        expo = sb("expo", [P, 8], F32)
        eps = sb("eps", [P, 8], F32)
        xh = sb("xh", [P, TILES + 1, DIM], F32)
        st1 = sb("st1", [P, TILES + 1, 6], F32)
        mv1 = sb("mv1", [P, TILES + 1, 2], F32)
        ve1 = sb("ve1", [P, TILES + 1], F32)
        rstd1 = sb("rstd1", [P, TILES + 1], F32)
        xn = xh
        xT_h, xT_l = sb("xT_h", [P, KC, HALO], F32R), sb("xT_l", [P, KC, HALO], F32R)
        qp = sb("qp", [P, GROUPS, 3, BLOCK], BF16)
        rq = sb("rq", [P, GROUPS, BLOCK], F32)
        kp = sb("kp", [GROUPS * HD, 3, HALO], BF16)
        rq_flat = rq[:, :, :].rearrange("p g t -> p (g t)")
        rk = rq_flat[0:GROUPS * HD, 0:HALO]
        rv = rq_flat[:, HALO:HALO + SUBS * GROUPS * HD].rearrange("p (c d) -> p c d", d=HD)
        rows64 = sb("rows64", [R0 + EXPERTS, HALO], F32)
        vT = rows64
        lT = rows64[R0:R0 + EXPERTS, 0:BLOCK]
        qst = [sb(f"qst{p}", [ROWS + MAXPARTS, SUBS, HEADS * SUB], BF16) for p in range(2)]
        kst = [sb(f"kst{p}", [ROWS + MAXPARTS, GROUPS, HALO], BF16) for p in range(2)]
        v3 = [sb(f"v3{p}", [P, SUBS * GROUPS, VW + 1], BF16) for p in range(2)]
        negmax = sb("negmax", [P, 2, PAIRS], F32)
        mp = sb("mp", [PAIRS, 2, MAXPARTS, P], BF16)
        prob = sb("prob", [P, GROUPS * 512], F32)
        prob_h, prob_l = sb("prob_h", [P, GROUPS * 512], F16), sb("prob_l", [P, GROUPS * 512], F16)
        upper_f = prob[:, 0:PAIRS * SUB // 2].bitcast(BF16).rearrange("p (a q) -> p a q", a=PAIRS)
        osum = sb("osum", [P, PAIRS, HD], F32)
        rden = sb("rden", [P, PAIRS], F32)
        o = sb("o", [P, 4, PAIRS * HD], F32)
        oT_h, oT_l = sb("oT_h", [P, 2, P], F32R), sb("oT_l", [P, 2, P], F32R)
        xres = sb("xres", [P, TILES, DIM], F32)
        xb = xres
        x1 = [sb(f"x1{p}", [P, TILES, DIM], F32) for p in range(2)]
        st2 = sb("st2", [P, 2, 6], F32)
        mv2 = sb("mv2", [P, 2, 2], F32)
        ve2 = sb("ve2", [P, 2], F32)
        rstd2 = sb("rstd2", [P, 2], F32)
        xn2 = sb("xn2", [P, 2, DIM], F32)
        x2_h = [sb(f"x2_h{p}", [P, KC, BLOCK], F32R) for p in range(2)]
        x2_l = [sb(f"x2_l{p}", [P, KC, BLOCK], F32R) for p in range(2)]
        lg = sb("lg", [P, TILES, EXPERTS + 8], F32)
        m8 = sb("m8", [P, TILES, 8], F32)
        ld = sb("ld", [P, TILES, EXPERTS], F32)
        le = sb("le", [P, TILES, EXPERTS], F32)
        rep = sb("rep", [P, TILES, EXPERTS + 8], F32)
        sel = sb("sel", [P, TILES, EXPERTS], F32)
        z = sb("z", [P, 6, TILES], F32)
        gate = [sb(f"gate{p}", [P, TILES, EXPERTS], F32) for p in range(2)]
        racc = [sb(f"racc{p}", [P, TILES], F32) for p in range(2)]
        etop = [sb(f"etop{p}", [P, TILES], F32) for p in range(2)]
        acc = sb("acc", [P, 2, DIM], F32)
        tmp = stage[:, 0:2, :]
        psum_p = stage[:, 2, :].rearrange("p (a n) -> p a n", a=2)
        y = stage[:, 3, :].rearrange("p (a n) -> p a n", a=2)
        acc_p = sb("acc_p", [P, DIM], F32)

        w_in = sem("w_in")
        b_in = sem("b_in")
        e_in = [sem(f"e_in{k}") for k in range(STAGES)]
        w_high = sem("w_high")
        w_split = sem("w_split")
        e_high = sem("e_high")
        e_split = sem("e_split")
        b_high = sem("b_high")
        zeroed = sem("zeroed")
        ones_up = sem("ones_up")
        masks_up = sem("masks_up")
        masks_ok = sem("masks_ok")
        x_in = sem("x_in")
        xres_in = sem("xres_in")
        ln1_stat, ln1_mv = sem("ln1_stat"), sem("ln1_mv")
        ln1_ve, ln1_rstd = sem("ln1_ve"), sem("ln1_rstd")
        xn_ready = sem("xn_ready")
        misc_full = sem("misc_full")
        misc_free = sem("misc_free")
        xT_high = sem("xT_high")
        q1_done, q2_done = sem("q1_done"), sem("q2_done")
        q3_done = sem("q3_done")
        q_out = sem("q_out")
        k1_done = sem("k1_done")
        k2_done = sem("k2_done")
        k3_done = sem("k3_done")
        k_out = sem("k_out")
        v1_done, v2_done = sem("v1_done"), sem("v2_done")
        v3_done = sem("v3_done")
        qk_in = sem("qk_in")
        s_full = sem("s_full")
        s_sel = sem("s_sel")
        max_done = sem("max_done")
        m1_done = sem("m1_done")
        m_in = [sem(f"m_in{p}") for p in range(2)]
        st_full = sem("st_full")
        exp_done = sem("exp_done")
        ph_done = sem("ph_done")
        pl_done = sem("pl_done")
        pv_full = sem("pv_full")
        o_parts = sem("o_parts")
        o_done = sem("o_done")
        oT_high = sem("oT_high")
        xb_ready = sem("xb_ready")
        ln2_stat, ln2_mv = sem("ln2_stat"), sem("ln2_mv")
        ln2_ve, ln2_rstd = sem("ln2_ve"), sem("ln2_rstd")
        xn2_ready = sem("xn2_ready")
        x2_high = sem("x2_high")
        r_seq = sem("r_seq")
        r_exp = sem("r_exp")
        gates_ready = sem("gates_ready")
        e_full = sem("e_full")
        e_read_act = sem("e_read_act")
        acc_seq = sem("acc_seq")
        p_sum = sem("p_sum")
        p_acc = sem("p_acc")
        f_seq = sem("f_seq")
        fin_done = sem("fin_done")
        y_done = sem("y_done")
        passed_dve, passed_pe = sem("passed_dve"), sem("passed_pe")
        y_out = [sem(f"y_out{p}") for p in range(2)]

        def use_no(tag, i, first, front):
            if first:
                return FRONT_USES.index(tag)
            uses = STEP_USES if front else LAST_USES
            return nth(i, len(STEP_USES), len(FRONT_USES) + uses.index(tag))

        def tile_rows(dram_block, n, rows=P):
            return dram_block[n * P:n * P + rows, :]

        block = ctx.enter_context(nc.Block())

        def program(e, step):
            for tag in FRONT_ORDER:
                step(tag, 0, 1, first=True, front=True, attend=False, experts=False)
            for tag in ORDER:
                step(tag, 0, 0, first=False, front=True, attend=True, experts=False)
            with e.Fori(0, BLOCKS // 2 - 1) as n:
                for half in range(2):
                    for tag in ORDER:
                        step(tag, n * 2 + (1 + half), (1 + half) % 2, first=False, front=True, attend=True, experts=True)
            for tag in ORDER:
                step(tag, BLOCKS - 1, (BLOCKS - 1) % 2, first=False, front=False, attend=True, experts=True)
            for tag in ORDER:
                if tag[0] == "M":
                    step(tag, BLOCKS, BLOCKS % 2, first=False, front=False, attend=False, experts=True)

        @block.sync
        def _(sp):
            sp.dma_start(stage[:, 0, :].rearrange("p (c n) -> p c n", c=KC),
                         wq.rearrange("(c p) n -> p c n", p=P)).then_inc(w_in, 16)
            kv = stage[:, 1, 0:KC * 64].rearrange("p (c n) -> p c n", c=KC)
            sp.dma_start(kv[:, :, 0:32], wk.rearrange("(c p) n -> p c n", p=P)).then_inc(w_in, 16)
            sp.dma_start(kv[:, :, 32:64], wv.rearrange("(c p) n -> p c n", p=P)).then_inc(w_in, 16)
            sp.dma_start(stage[:, 2, :].rearrange("p (c n) -> p c n", c=2), wo.rearrange("(c p) n -> p c n", p=P)).then_inc(w_in, 16)
            sp.dma_start(stage[:, 3, 0:KC * EXPERTS].rearrange("p (c n) -> p c n", c=KC),
                         rwt.rearrange("(c p) n -> p c n", p=P)).then_inc(w_in, 16)

            def step(tag, i, par, first, front, attend, experts):
                kind, k = tag
                f = 0 if first else i + 1
                pf = 0 if first else 1 - par
                if front and tag == (("LN1", 0) if first else ("S", 0)):
                    if not first:
                        before = 3 if isinstance(i, int) and i == 0 else use_no(("T", 2), i - 1, False, True) + 1
                        sp.wait_ge(misc_free, before)
                    sp.dma_start(xh[:, 0:TILES, :], x_halo[f, 0:BLOCK, :].rearrange("(t p) d -> p t d", p=P)).then_inc(x_in, 16)
                    sp.dma_start(xh[0:2 * HALF, TILES, :], x_halo[f, BLOCK:HALO, :]).then_inc(x_in, 16)
                if attend and kind == "S" and k == 1:
                    if not (isinstance(i, int) and i == 0):
                        sp.wait_ge(misc_free, use_no(("WO", TILES - 1), i - 1, False, True) + 1)
                    sp.dma_start(xres[:, :, :], x_halo[i, HALF:HALF + BLOCK, :].rearrange("(t p) d -> p t d", p=P)).then_inc(xres_in, 16)
                if attend and kind == "MT":
                    sp.wait_ge(misc_free, use_no(tag, i, first, front) + 1)
                    for part in range(MAXPARTS):
                        sp.dma_start(qst[par][ROWS + part:ROWS + part + 1, k, :], mp[:, k % 2, part, :]).then_inc(m_in[k % 2], 16)
                if front and kind == "Qb":
                    sp.wait_ge(q3_done, nth(f, 2, k + 1))
                    sp.dma_start(q_dram[f, k].rearrange("s u p q -> p (s u) q"),
                                 qp[:, k, :, :].rearrange("p s (u q) -> p (s u) q", q=SUB)).then_inc(q_out, 16)
                    if k == 1:
                        sp.wait_ge(q_out, nth(f, 32, 32))
                        for s in range(SLOTS_QK):
                            for g in range(GROUPS):
                                sp.dma_start(qst[pf][s * HD:(s + 1) * HD, :, g * 512:(g + 1) * 512],
                                             q_dram[f, g, Q_PART[s]].rearrange("u (d h) q -> d u (h q)", d=HD)).then_inc(qk_in, 16)
                if front and kind == "VTb":
                    sp.wait_ge(k3_done, nth(f, 1, 1))
                    sp.dma_start(k_dram[f].rearrange("s p t -> p s t"), kp[:, :, :]).then_inc(k_out, 16)
                    sp.wait_ge(k_out, nth(f, 16, 16))
                    for s in range(SLOTS_QK):
                        sp.dma_start(kst[pf][s * HD:(s + 1) * HD, :, :],
                                     k_dram[f, K_PART[s], :, :].rearrange("(g d) t -> d g t", d=HD)).then_inc(qk_in, 16)
                if kind == "M" and not experts and k % 2 == 0:
                    ex = k // 2
                    if ex >= STAGES:
                        sp.wait_ge(e_split, ex - STAGES + 1)
                    else:
                        sp.wait_ge(w_split, 4)
                    sp.dma_start(stage[:, ex % STAGES, :].rearrange("p (c n) -> p c n", c=KC),
                                 ew[ex].rearrange("(c p) n -> p c n", p=P)).then_inc(e_in[ex % STAGES], 16)

            program(sp, step)

        @block.gpsimd
        def _(pool):
            for g in range(GROUPS):
                pool.dma_start(bq_c[:, g:g + 1], bq.rearrange("(n a) -> n a", a=1)[g * P:(g + 1) * P, :]).then_inc(b_in, 16)
            pool.dma_start(bkv[:, 0:32], bk.rearrange("(a n) -> a n", a=1)).then_inc(b_in, 16)
            pool.dma_start(bkv[:, 32:64], bv.rearrange("(a n) -> a n", a=1)).then_inc(b_in, 16)
            pool.dma_start(bo_b[:, :], bo.rearrange("(a n) -> a n", a=1).broadcast_to([P, DIM])).then_inc(b_in, 16)
            pool.dma_start(rb_c[R0:R0 + EXPERTS, :], rb.rearrange("(n a) -> n a", a=1)).then_inc(b_in, 16)
            nc.gpsimd.memset(ident[:, :], 0.0).then_inc(ones_up, 1)
            nc.gpsimd.memset(ident_b[:, :], 0.0).then_inc(ones_up, 1)
            nc.gpsimd.memset(far[:, :, :], 0.0).then_inc(ones_up, 1)
            nc.gpsimd.memset(upper_f[:, :, :], 1.0).then_inc(ones_up, 1)
            nc.gpsimd.memset(expo[:, :], -0.5).then_inc(ones_up, 1)
            nc.gpsimd.memset(eps[:, :], EPS_LN).then_inc(ones_up, 1)
            nc.gpsimd.memset(acc_p[:, :], 0.0).then_inc(p_sum, 1)
            pool.wait_ge(ones_up, 6)
            for t in (ident, ident_b):
                nc.gpsimd.affine_select(out=t[:, :], in_=t[:, :], compare_op=ALU.not_equal, fill=1.0, base=0,
                                        pattern=[[-1, P]], channel_multiplier=1).then_inc(masks_up, 1)
            nc.gpsimd.affine_select(out=far[:, :, :], in_=far[:, :, :], compare_op=ALU.is_ge, fill=FAR, base=0,
                                    pattern=[[0, PER_GROUP], [-1, SUB]], channel_multiplier=1).then_inc(masks_up, 1)
            pool.wait_ge(masks_up, 3)
            nc.gpsimd.affine_select(out=far[:, :, :], in_=far[:, :, :], compare_op=ALU.is_ge, fill=FAR, base=WINDOW - 1,
                                    pattern=[[0, PER_GROUP], [1, SUB]], channel_multiplier=-1).then_inc(masks_up, 1)
            for r in range(2):
                pool.wait_ge(masks_up, 4 + r)
                part = upper_f[r * SUB:(r + 1) * SUB, :, :]
                nc.gpsimd.affine_select(out=part, in_=part, compare_op=ALU.is_gt, fill=0.0, base=0,
                                        pattern=[[0, PAIRS], [-1, SUB]], channel_multiplier=1).then_inc(masks_up, 1)

            def step(tag, i, par, first, front, attend, experts):
                kind, k = tag
                f = 0 if first else i + 1
                j, pj = i - 1, 1 - par
                if front and kind == "LN1":
                    pool.wait_ge(ln1_mv, nth(f, 1, 1))
                    nc.gpsimd.tensor_tensor(ve1[:, :], mv1[:, :, 1], eps[:, 0:TILES + 1], ALU.add).then_inc(ln1_ve, 1)
                    pool.wait_ge(ln1_ve, nth(f, 1, 1))
                    nc.gpsimd.tensor_tensor(rstd1[:, :], ve1[:, :], expo[:, 0:TILES + 1], ALU.pow).then_inc(ln1_rstd, 1)
                if attend and tag == ("PV", 0):
                    pool.wait_ge(xres_in, nth(i, 16, 16))
                    if isinstance(i, int) and i == 0:
                        pool.wait_ge(b_in, 16 * 6)
                    nc.gpsimd.tensor_tensor(xb[:, :, :], xres[:, :, :], bo_b[:, :].rearrange("p (a n) -> p a n", a=1).broadcast_to([P, TILES, DIM]),
                                            ALU.add).then_inc(xb_ready, 1)
                if attend and kind == "ST":
                    pool.wait_ge(ph_done, nth(i, SUBS, k + 1))
                    nc.gpsimd.tensor_tensor(prob_l[:, :], prob[:, :], prob_h[:, :], ALU.subtract).then_inc(pl_done, 1)
                if attend and kind == "WO":
                    pool.wait_ge(ln2_mv, nth(i, TILES, k + 1))
                    nc.gpsimd.tensor_tensor(ve2[:, k % 2:k % 2 + 1], mv2[:, k % 2, 1:2], eps[:, 0:1], ALU.add).then_inc(ln2_ve, 1)
                    pool.wait_ge(ln2_ve, nth(i, TILES, k + 1))
                    nc.gpsimd.tensor_tensor(rstd2[:, k % 2:k % 2 + 1], ve2[:, k % 2:k % 2 + 1], expo[:, 0:1], ALU.pow).then_inc(ln2_rstd, 1)
                if experts and kind == "M":
                    t, g = k // EG, k % EG
                    if g in BY_ACT:
                        a = BY_ACT.index(g)
                        pool.wait_ge(e_read_act, nth(j, TILES * len(BY_ACT), t * len(BY_ACT) + a + 1))
                        nc.gpsimd.tensor_tensor(psum_p[:, a, :], tmp[:, a, 0:DIM], tmp[:, a, DIM:2 * DIM], ALU.add).then_inc(p_sum, 1)
                    if g == EG - 1:
                        pool.wait_ge(p_sum, SUM_0 + nth(j, 2 * TILES, 2 * t + 2))
                        if not (isinstance(j, int) and j == 0 and t == 0):
                            pool.wait_ge(y_done, nth(j, TILES, t))
                        nc.gpsimd.tensor_tensor(acc_p[:, :], psum_p[:, 0, :], psum_p[:, 1, :], ALU.add).then_inc(p_acc, 1)
                        pool.wait_ge(y_done, nth(j, TILES, t + 1))
                        pool.dma_start(out[j, t * P:(t + 1) * P, :], y[:, t % 2, :]).then_inc(y_out[t % 2], 16)

            program(pool, step)
            for p in range(2):
                pool.wait_ge(y_out[p], 16 * BLOCKS * TILES // 2)

        @block.scalar
        def _(act):
            act.wait_ge(w_in, 16 * 5)
            act.wait_ge(zeroed, 1)
            for dst, src in ((wq_h[:, :, :], stage[:, 0, :].rearrange("p (c n) -> p c n", c=KC)),
                             (wkv_h[:, :, 0:64], stage[:, 1, 0:KC * 64].rearrange("p (c n) -> p c n", c=KC)),
                             (wo_h[:, :, :], stage[:, 2, :].rearrange("p (c n) -> p c n", c=2)),
                             (wkv_h[:, :, R0:R0 + EXPERTS], stage[:, 3, 0:KC * EXPERTS].rearrange("p (c n) -> p c n", c=KC))):
                nc.scalar.activation(dst, src, ACT.Copy).then_inc(w_high, 1)
            act.wait_ge(b_in, 16 * 6)
            nc.scalar.activation(bkv_h[:, 0:64], bkv[:, :], ACT.Copy).then_inc(b_high, 1)

            def step(tag, i, par, first, front, attend, experts):
                kind, k = tag
                f = 0 if first else i + 1
                pf = 0 if first else 1 - par
                j, pj = i - 1, 1 - par
                if kind in USES and (front if kind in IN_FRONT else attend):
                    act_waits_misc = kind not in ("MT", "WO", "LG")
                    if act_waits_misc:
                        act.wait_ge(misc_full, use_no(tag, i, first, front) + 1)
                if front and kind == "T":
                    if k < KC:
                        nc.scalar.activation(xT_h[:, k, 0:BLOCK], misc[:, :], ACT.Copy).then_inc(xT_high, 1)
                    else:
                        nc.scalar.activation(xT_h[:, :, BLOCK:HALO],
                                             misc[:, 0:KC * 2 * HALF].rearrange("p (c n) -> p c n", c=KC), ACT.Copy).then_inc(xT_high, 1)
                if front and kind == "Q":
                    if not first:
                        act.wait_ge(q_out, nth(f, 32, 0))
                    nc.scalar.activation(qp[:, k, 0, :], misc[:, :], ACT.Identity, bias=bq_c[:, k:k + 1]).then_inc(q1_done, 1)
                    act.wait_ge(misc_free, use_no(tag, i, first, front) + 1)
                    nc.scalar.activation(qp[:, k, 1, :], rq[:, k, :], ACT.Copy).then_inc(q2_done, 1)
                if front and kind == "KV":
                    h = HALO // 2
                    if not first:
                        act.wait_ge(k_out, nth(f, 16, 0))
                    nc.scalar.activation(kp[:, 0, k * h:(k + 1) * h], misc[0:32, 0:h], ACT.Copy)
                    nc.scalar.activation(vT[32:64, k * h:(k + 1) * h], misc[32:64, 0:h], ACT.Copy).then_inc(k1_done, 1)
                    if k == 1:
                        act.wait_ge(misc_free, use_no(tag, i, first, front) + 1)
                        nc.scalar.activation(kp[:, 1, :], rk[:, :], ACT.Copy).then_inc(k2_done, 1)
                if front and kind == "VT":
                    nc.scalar.activation(v3[pf][:, :, 0:HD], misc[:, 0:SUBS * 32].rearrange("p (c d) -> p c d", d=HD),
                                         ACT.Copy).then_inc(v1_done, 1)
                    act.wait_ge(misc_free, use_no(tag, i, first, front) + 1)
                    nc.scalar.activation(v3[pf][:, :, HD:2 * HD], rv[:, :, :], ACT.Copy).then_inc(v2_done, 1)
                if attend and kind == "ST":
                    act.wait_ge(st_full, nth(i, SUBS, k + 1))
                    if not (isinstance(i, int) and i == 0 and k == 0):
                        act.wait_ge(pl_done, nth(i, SUBS, k))
                    nc.scalar.activation(prob[:, :], st_ps[:, :, :].rearrange("p g n -> p (g n)"), ACT.Exp).then_inc(exp_done, 1)
                    act.wait_ge(exp_done, nth(i, SUBS, k + 1))
                    if not (isinstance(i, int) and i == 0 and k == 0):
                        act.wait_ge(pv_full, nth(i, SUBS, k))
                    nc.scalar.activation(prob_h[:, :], prob[:, :], ACT.Copy).then_inc(ph_done, 1)
                if attend and kind == "OT":
                    nc.scalar.activation(oT_h[:, :, :].rearrange("p r (s q) -> p s r q", s=2),
                                         misc[:, 0:2 * P].rearrange("p (s r q) -> p s r q", s=2, r=2), ACT.Copy).then_inc(oT_high, 1)
                if attend and kind == "X2T":
                    nc.scalar.activation(x2_h[par][:, :, k * P:(k + 1) * P], misc[:, 0:KC * P].rearrange("p (c n) -> p c n", c=KC),
                                         ACT.Copy).then_inc(x2_high, 1)
                if attend and kind == "LT":
                    nc.scalar.activation(lT[:, :], misc[R0:R0 + EXPERTS, :], ACT.Identity, bias=rb_c[R0:R0 + EXPERTS, 0:1]).then_inc(misc_free, 1)
                if attend and kind == "LG":
                    act.wait_ge(r_seq, nth(i, R_STEPS, 3))
                    nc.scalar.activation(le[:, :, :], ld[:, :, :], ACT.Exp).then_inc(r_exp, 1)
                if kind == "M" and experts:
                    t, g = k // EG, k % EG
                    if g in BY_ACT:
                        a = BY_ACT.index(g)
                        act.wait_ge(e_full, nth(j, TILES * EG, k + 1))
                        act.wait_ge(gates_ready, nth(j, 1, 1))
                        if not (isinstance(j, int) and j == 0 and t == 0):
                            act.wait_ge(p_sum, SUM_0 + nth(j, 2 * TILES, 2 * t - 1 + a))
                        for q in range(2):
                            last = nc.scalar.activation(tmp[:, a, q * DIM:(q + 1) * DIM], e_ps[:, k % 2, q * DIM:(q + 1) * DIM],
                                                        ACT.Copy, scale=gate[pj][:, t, 2 * g + q:2 * g + q + 1])
                        last.then_inc(e_read_act, 1)
                    if g == EG - 1:
                        act.wait_ge(fin_done, nth(j, TILES, t + 1))
                        if not (isinstance(j, int) and j == 0 and t < 2):
                            act.wait_ge(y_out[t % 2], nth(j, 16 * TILES // 2, 16 * (t // 2)))
                        nc.scalar.activation(y[:, t % 2, :], acc_p[:, :], ACT.Identity, bias=etop[pj][:, t:t + 1]).then_inc(y_done, 1)
                if kind == "M" and not experts and k % 2 == 1:
                    ex = k // 2
                    act.wait_ge(e_in[ex % STAGES], 16 * (ex // STAGES + 1))
                    nc.scalar.activation(we_h[:, :, ex, :], stage[:, ex % STAGES, :].rearrange("p (c n) -> p c n", c=KC),
                                         ACT.Copy).then_inc(e_high, 1)

            program(act, step)

        @block.vector
        def _(dve):
            for t in (wkv_h, wkv_l):
                nc.vector.memset(t[:, :, :].bitcast(F32), 0.0)
            nc.vector.memset(bkv_h[:, :].bitcast(F32), 0.0)
            nc.vector.memset(bkv_l[:, :].bitcast(F32), 0.0).then_inc(zeroed, 1)
            nc.vector.memset(valid[:, :].bitcast(F32), 1.0).then_inc(zeroed, 1)
            nc.vector.memset(xh[2 * HALF:P, TILES, :], 0.0)
            nc.vector.memset(lg[:, :, EXPERTS:], -HUGE)
            for p in range(2):
                nc.vector.memset(kst[p][ROWS:ROWS + MAXPARTS, :, :], 1.0)
                nc.vector.memset(v3[p][:, :, 3 * HD:VW + 1], 1.0)
            for q in range(2):
                nc.vector.memset(acc[:, q, :], 0.0).then_inc(acc_seq, 1)
            dve.wait_ge(zeroed, 2)
            nc.vector.memset(valid[:, 0:HALF].bitcast(F32), 0.0)
            nc.vector.memset(valid[:, HALO:HALO + HALF].bitcast(F32), 0.0).then_inc(zeroed, 1)
            for n, (dst, src, high) in enumerate((
                    (wq_l[:, :, :], stage[:, 0, :].rearrange("p (c n) -> p c n", c=KC), wq_h[:, :, :]),
                    (wkv_l[:, :, 0:64], stage[:, 1, 0:KC * 64].rearrange("p (c n) -> p c n", c=KC), wkv_h[:, :, 0:64]),
                    (wo_l[:, :, :], stage[:, 2, :].rearrange("p (c n) -> p c n", c=2), wo_h[:, :, :]),
                    (wkv_l[:, :, R0:R0 + EXPERTS], stage[:, 3, 0:KC * EXPERTS].rearrange("p (c n) -> p c n", c=KC), wkv_h[:, :, R0:R0 + EXPERTS]))):
                dve.wait_ge(w_high, n + 1)
                nc.vector.tensor_tensor(dst, src, high.bitcast(F32), ALU.subtract).then_inc(w_split, 1)
            dve.wait_ge(b_high, 1)
            nc.vector.tensor_tensor(bkv_l[:, 0:64], bkv[:, :], bkv_h[:, 0:64].bitcast(F32), ALU.subtract).then_inc(b_high, 1)
            dve.wait_ge(masks_up, 6)
            nc.vector.tensor_copy(upper[:, :, :], upper_f[:, :, :]).then_inc(masks_ok, 1)
            dve.wait_ge(masks_ok, 1)

            def settled():
                dve.sem_inc(passed_dve, 1)

            def ln1(f, first):
                dve.wait_ge(x_in, nth(f, 32, 32))
                for n in range(TILES + 1):
                    last = nc.vector.bn_stats(st1[:, n, :], xh[:, n, :])
                last.then_inc(ln1_stat, 1)
                dve.wait_ge(ln1_stat, nth(f, 1, 1))
                settled()
                for n in range(TILES + 1):
                    last = nc.vector.bn_aggr(mv1[:, n, :], st1[:, n, :])
                last.then_inc(ln1_mv, 1)
                dve.wait_ge(ln1_rstd, nth(f, 1, 1))
                for n in range(TILES + 1):
                    last = nc.vector.tensor_scalar(xn[:, n, :], xh[:, n, :], mv1[:, n, 0:1], rstd1[:, n:n + 1],
                                                   ALU.subtract, ALU.mult)
                last.then_inc(xn_ready, 1)

            def router(i, par):
                seq = [0]

                def link(ins):
                    seq[0] += 1
                    ins.then_inc(r_seq, 1)
                    dve.wait_ge(r_seq, nth(i, R_STEPS, seq[0]))

                def wide(v):
                    return v.rearrange("p (t a) -> p t a", a=1).broadcast_to([P, TILES, EXPERTS])

                logits = lg[:, :, 0:EXPERTS]
                dve.wait_ge(misc_free, use_no(("LG", 0), i, False, not (isinstance(i, int) and i == BLOCKS - 1)) + 1)
                settled()
                for t in range(TILES):
                    last = nc.vector.max(m8[:, t, :], lg[:, t, 0:EXPERTS])
                link(last)
                link(nc.vector.tensor_copy(z[:, 0, :], m8[:, :, 0]))
                link(nc.vector.tensor_tensor(ld[:, :, :], logits, wide(z[:, 0, :]), ALU.subtract))
                link(nc.vector.memset(m8[:, :, TOP_K:8], -HUGE))
                settled()
                for t in range(TILES):
                    last = nc.vector.match_replace(rep[:, t, :], m8[:, t, :], lg[:, t, :], HUGE)
                link(last)
                link(nc.vector.tensor_scalar(sel[:, :, :], rep[:, :, 0:EXPERTS], HUGE, None, ALU.is_equal))
                dve.wait_ge(r_exp, nth(i, 1, 1))
                link(nc.vector.tensor_reduce(z[:, 1, :], le[:, :, :], AX.X, ALU.add))
                link(nc.vector.reciprocal(z[:, 2, :], z[:, 1, :]))
                link(nc.vector.tensor_tensor(ld[:, :, :], le[:, :, :], wide(z[:, 2, :]), ALU.mult))
                link(nc.vector.tensor_tensor(sel[:, :, :], sel[:, :, :], ld[:, :, :], ALU.mult))
                link(nc.vector.tensor_reduce(z[:, 3, :], sel[:, :, :], AX.X, ALU.add))
                link(nc.vector.tensor_scalar(z[:, 3, :], z[:, 3, :], EPS_GATE, None, ALU.add))
                link(nc.vector.reciprocal(z[:, 4, :], z[:, 3, :]))
                link(nc.vector.tensor_tensor(gate[par][:, :, :], sel[:, :, :], wide(z[:, 4, :]), ALU.mult))
                link(nc.vector.tensor_reduce(z[:, 5, :], gate[par][:, :, :], AX.X, ALU.add))
                link(nc.vector.tensor_scalar(z[:, 0, :], z[:, 5, :], EPS_GATE, None, ALU.max))
                nc.vector.tensor_scalar(etop[par][:, :], z[:, 5, :], EPS_GATE, None, ALU.mult)
                nc.vector.reciprocal(racc[par][:, :], z[:, 0, :]).then_inc(gates_ready, 1)
                assert seq[0] == R_STEPS, seq

            def step(tag, i, par, first, front, attend, experts):
                kind, k = tag
                f = 0 if first else i + 1
                pf = 0 if first else 1 - par
                j, pj = i - 1, 1 - par
                use = use_no(tag, i, first, front) if kind in USES and (front if kind in IN_FRONT else attend) else None
                if front and kind == "LN1":
                    ln1(f, first)
                if front and kind == "T":
                    dve.wait_ge(misc_full, use + 1)
                    dve.wait_ge(xT_high, nth(f, 3, k + 1))
                    if k < KC:
                        d, s, h = xT_l[:, k, 0:BLOCK], misc[:, :], xT_h[:, k, 0:BLOCK]
                    else:
                        d, h = xT_l[:, :, BLOCK:HALO], xT_h[:, :, BLOCK:HALO]
                        s = misc[:, 0:KC * 2 * HALF].rearrange("p (c n) -> p c n", c=KC)
                    nc.vector.tensor_tensor(d, s, h.bitcast(F32), ALU.subtract).then_inc(misc_free, 1)
                if front and kind == "Q":
                    dve.wait_ge(misc_full, use + 1)
                    dve.wait_ge(q1_done, nth(f, 2, k + 1))
                    nc.vector.scalar_tensor_tensor(out=rq[:, k, :], in0=misc[:, :], scalar=bq_c[:, k:k + 1],
                                                   in1=qp[:, k, 0, :], op0=ALU.add, op1=ALU.subtract).then_inc(misc_free, 1)
                if front and kind == "Qb":
                    dve.wait_ge(q2_done, nth(f, 2, k + 1))
                    nc.vector.tensor_tensor(qp[:, k, 2, :], rq[:, k, :], qp[:, k, 1, :], ALU.subtract).then_inc(q3_done, 1)
                if front and kind == "KV":
                    h = HALO // 2
                    dve.wait_ge(misc_full, use + 1)
                    dve.wait_ge(k1_done, nth(f, 2, k + 1))
                    dve.wait_ge(q3_done, nth(f, 2, 2))
                    nc.vector.tensor_tensor(rk[:, k * h:(k + 1) * h], misc[0:32, 0:h], kp[:, 0, k * h:(k + 1) * h],
                                            ALU.subtract).then_inc(misc_free, 1)
                if front and kind == "KVb":
                    dve.wait_ge(k2_done, nth(f, 1, 1))
                    nc.vector.tensor_tensor(kp[:, 2, :], rk[:, :], kp[:, 1, :], ALU.subtract).then_inc(k3_done, 1)
                if front and kind == "VT":
                    dve.wait_ge(misc_full, use + 1)
                    dve.wait_ge(v1_done, nth(f, 1, 1))
                    nc.vector.tensor_tensor(rv[:, :, :], misc[:, 0:SUBS * 32].rearrange("p (c d) -> p c d", d=HD),
                                            v3[pf][:, :, 0:HD], ALU.subtract).then_inc(misc_free, 1)
                if front and kind == "VTb":
                    dve.wait_ge(v2_done, nth(f, 1, 1))
                    nc.vector.tensor_tensor(v3[pf][:, :, 2 * HD:3 * HD], rv[:, :, :], v3[pf][:, :, HD:2 * HD],
                                            ALU.subtract).then_inc(v3_done, 1)
                if attend and kind == "S":
                    dve.wait_ge(s_full, nth(i, SUBS, k + 1))
                    settled()
                    nc.vector.copy_predicated(s_ps[:, :, 0:SUB], upper[:, :, :], s_ps[:, :, SUB:2 * SUB]).then_inc(s_sel, 1)
                    dve.wait_ge(s_sel, nth(i, SUBS, k + 1))
                    nc.vector.tensor_reduce(negmax[:, k % 2, :], s_ps[:, :, 0:SUB], AX.X, ALU.max, negate=True).then_inc(max_done, 1)
                if attend and kind == "MT":
                    dve.wait_ge(misc_full, use + 1)
                    if not (isinstance(i, int) and i == 0 and k < 2):
                        dve.wait_ge(m_in[k % 2], nth(i, 32 * SUBS // 2, 32 * (k // 2)))
                    nc.vector.tensor_copy(mp[:, k % 2, 0, :], misc[0:PAIRS, 0:P]).then_inc(m1_done, 1)
                    dve.wait_ge(m1_done, nth(i, SUBS, k + 1))
                    nc.vector.tensor_tensor(mp[:, k % 2, 1, :], misc[0:PAIRS, 0:P], mp[:, k % 2, 0, :], ALU.subtract).then_inc(misc_free, 1)
                if attend and kind == "PV":
                    dve.wait_ge(pv_full, nth(i, SUBS, k + 1))
                    part = pv_ps[:, 0:PAIRS * VW].rearrange("p (a w) -> p a w", w=VW)
                    nc.vector.tensor_reduce(osum[:, :, :], part[:, :, 0:3 * HD].rearrange("p a (s d) -> p a d s", s=3),
                                            AX.X, ALU.add)
                    nc.vector.reciprocal(rden[:, :], part[:, :, 3 * HD]).then_inc(o_parts, 1)
                    dve.wait_ge(o_parts, nth(i, SUBS, k + 1))
                    nc.vector.tensor_tensor(o[:, k % 4, :].rearrange("p (a d) -> p a d", d=HD), osum[:, :, :],
                                            rden[:, :].rearrange("p (a d) -> p a d", d=1).broadcast_to([P, PAIRS, HD]), ALU.mult).then_inc(o_done, 1)
                if attend and kind == "OT":
                    dve.wait_ge(misc_full, use + 1)
                    dve.wait_ge(oT_high, nth(i, TILES, k + 1))
                    nc.vector.tensor_tensor(oT_l[:, :, :].rearrange("p r (s q) -> p s r q", s=2),
                                            misc[:, 0:2 * P].rearrange("p (s r q) -> p s r q", s=2, r=2),
                                            oT_h[:, :, :].bitcast(F32).rearrange("p r (s q) -> p s r q", s=2), ALU.subtract).then_inc(misc_free, 1)
                if attend and kind == "WO":
                    dve.wait_ge(misc_full, use + 1)
                    dve.wait_ge(xb_ready, nth(i, 1, 1))
                    nc.vector.tensor_tensor(x1[par][:, k, :], misc[:, 0:DIM], xb[:, k, :], ALU.add).then_inc(misc_free, 1)
                    dve.wait_ge(misc_free, use + 1)
                    nc.vector.bn_stats(st2[:, k % 2, :], x1[par][:, k, :]).then_inc(ln2_stat, 1)
                    dve.wait_ge(ln2_stat, nth(i, TILES, k + 1))
                    settled()
                    nc.vector.bn_aggr(mv2[:, k % 2, :], st2[:, k % 2, :]).then_inc(ln2_mv, 1)
                if attend and kind == "X2T":
                    dve.wait_ge(ln2_rstd, nth(i, TILES, k + 1))
                    nc.vector.tensor_scalar(xn2[:, k % 2, :], x1[par][:, k, :], mv2[:, k % 2, 0:1], rstd2[:, k % 2:k % 2 + 1],
                                            ALU.subtract, ALU.mult).then_inc(xn2_ready, 1)
                    dve.wait_ge(misc_full, use + 1)
                    dve.wait_ge(x2_high, nth(i, TILES, k + 1))
                    nc.vector.tensor_tensor(x2_l[par][:, :, k * P:(k + 1) * P], misc[:, 0:KC * P].rearrange("p (c n) -> p c n", c=KC),
                                            x2_h[par][:, :, k * P:(k + 1) * P].bitcast(F32), ALU.subtract).then_inc(misc_free, 1)
                if attend and kind == "LG":
                    dve.wait_ge(misc_full, use + 1)
                    nc.vector.tensor_copy(lg[:, :, 0:EXPERTS], misc[:, 0:TILES * EXPERTS].rearrange("p (t n) -> p t n", n=EXPERTS)).then_inc(misc_free, 1)
                    router(i, par)
                if kind == "M" and experts:
                    t, g = k // EG, k % EG
                    if g in BY_DVE:
                        a = BY_DVE.index(g)
                        dve.wait_ge(e_full, nth(j, TILES * EG, k + 1))
                        if k == 0:
                            dve.wait_ge(gates_ready, nth(j, 1, 1))
                        for q in range(2):
                            scale = gate[pj][:, t, 2 * g + q:2 * g + q + 1]
                            src = e_ps[:, k % 2, q * DIM:(q + 1) * DIM]
                            done = 2 * (t * len(BY_DVE) + a) + q
                            if a == 0:
                                ins = nc.vector.tensor_scalar(acc[:, q, :], src, scale, None, ALU.mult)
                            else:
                                dve.wait_ge(acc_seq, ACC_0 + nth(j, 2 * TILES * len(BY_DVE), done - 1))
                                ins = nc.vector.scalar_tensor_tensor(out=acc[:, q, :], in0=src, scalar=scale, in1=acc[:, q, :],
                                                                     op0=ALU.mult, op1=ALU.add)
                            ins.then_inc(acc_seq, 1)
                    if g == EG - 1:
                        dve.wait_ge(acc_seq, ACC_0 + nth(j, 2 * TILES * len(BY_DVE), 2 * (t + 1) * len(BY_DVE)))
                        dve.wait_ge(p_acc, nth(j, TILES, t + 1))
                        for q in range(2):
                            nc.vector.tensor_tensor(acc_p[:, :], acc_p[:, :], acc[:, q, :], ALU.add).then_inc(f_seq, 1)
                            dve.wait_ge(f_seq, nth(j, 2 * TILES, 2 * t + 1 + q))
                        nc.vector.scalar_tensor_tensor(out=acc_p[:, :], in0=acc_p[:, :], scalar=racc[pj][:, t:t + 1], in1=x1[pj][:, t, :],
                                                       op0=ALU.mult, op1=ALU.add).then_inc(fin_done, 1)
                if kind == "M" and not experts and k % 2 == 1:
                    ex = k // 2
                    dve.wait_ge(e_high, ex + 1)
                    nc.vector.tensor_tensor(we_l[:, :, ex, :], stage[:, ex % STAGES, :].rearrange("p (c n) -> p c n", c=KC),
                                            we_h[:, :, ex, :].bitcast(F32), ALU.subtract).then_inc(e_split, 1)

            program(dve, step)

        @block.tensor
        def _(pe):
            pe.wait_ge(masks_up, 6)
            pe.wait_ge(w_split, 4)
            pe.wait_ge(b_high, 2)
            pe.wait_ge(zeroed, 3)

            def three(dst, pairs, close=True, opened=False):
                n = 0
                for w_high_, w_low_, x_high_, x_low_ in pairs:
                    for w, x in ((w_high_, x_high_), (w_high_, x_low_), (w_low_, x_high_)):
                        last = nc.tensor.matmul(dst, w, x, start=(n == 0 and not opened), stop=(close and n == 3 * len(pairs) - 1))
                        n += 1
                return last

            def step(tag, i, par, first, front, attend, experts):
                kind, k = tag
                f = 0 if first else i + 1
                pf = 0 if first else 1 - par
                j, pj = i - 1, 1 - par
                if kind in USES and (front if kind in IN_FRONT else attend):
                    use = use_no(tag, i, first, front)
                    if kind == "T" and k == 0:
                        pe.wait_ge(xn_ready, nth(f, 1, 1))
                    if kind == "MT":
                        pe.wait_ge(max_done, nth(i, SUBS, k + 1))
                    if kind == "OT":
                        pe.wait_ge(o_done, nth(i, SUBS, 2 * k + 2))
                    if kind == "X2T":
                        pe.wait_ge(xn2_ready, nth(i, TILES, k + 1))
                    if not (isinstance(use, int) and use == 0):
                        pe.wait_ge(misc_free, use)
                    if tag in (("T", KC), ("VT", 0), ("LG", 0)):
                        pe.sem_inc(passed_pe, 1)
                if front and kind == "T":
                    if k < KC:
                        for n in range(TILES):
                            last = nc.tensor.transpose(misc[:, n * P:(n + 1) * P], xn[:, n, k * P:(k + 1) * P], ident[:, :])
                    else:
                        w = 2 * HALF
                        for c in range(KC):
                            last = nc.tensor.transpose(misc[:, c * w:(c + 1) * w], xn[0:w, TILES, c * P:(c + 1) * P], ident[0:w, 0:w])
                    last.then_inc(misc_full, 1)
                if front and kind == "Q":
                    three(misc[:, :], [(wq_h[:, c, k * P:(k + 1) * P], wq_l[:, c, k * P:(k + 1) * P],
                                        xT_h[:, c, HALF:HALF + BLOCK], xT_l[:, c, HALF:HALF + BLOCK]) for c in range(KC)]).then_inc(misc_full, 1)
                if front and kind == "KV":
                    h = HALO // 2
                    cols = slice(k * h, (k + 1) * h)
                    three(misc[:, 0:h], [(wkv_h[:, c, :], wkv_l[:, c, :], xT_h[:, c, cols], xT_l[:, c, cols]) for c in range(KC)], close=False)
                    nc.tensor.matmul(misc[:, 0:h], bkv_h[:, :], valid[:, pf * HALF + k * h:pf * HALF + (k + 1) * h], start=False, stop=False)
                    nc.tensor.matmul(misc[:, 0:h], bkv_l[:, :], valid[:, pf * HALF + k * h:pf * HALF + (k + 1) * h], start=False, stop=True).then_inc(misc_full, 1)
                if front and kind == "VT":
                    for c in range(SUBS):
                        last = nc.tensor.transpose(misc[:, c * 32:(c + 1) * 32], vT[32:64, c * SUB:c * SUB + P], ident[32:64, 32:64])
                    last.then_inc(misc_full, 1)
                if attend and kind == "S":
                    if k == 0:
                        pe.wait_ge(qk_in, nth(i, QK_LOADS, QK_LOADS))
                    if not (isinstance(i, int) and i == 0 and k == 0):
                        pe.wait_ge(max_done, nth(i, SUBS, k))
                    for a in range(PAIRS):
                        last = nc.tensor.matmul(s_ps[:, a, :], qst[par][0:ROWS, k, a * P:(a + 1) * P],
                                                kst[par][0:ROWS, a // (PAIRS // 2), k * SUB:k * SUB + P], start=True, stop=True)
                    last.then_inc(s_full, 1)
                if attend and kind == "MT":
                    nc.tensor.transpose(misc[0:PAIRS, 0:P], negmax[:, k % 2, :], ident[:, :]).then_inc(misc_full, 1)
                if attend and kind == "ST":
                    pe.wait_ge(m_in[k % 2], nth(i, 32 * SUBS // 2, 32 * (k // 2 + 1)))
                    if not (isinstance(i, int) and i == 0 and k == 0):
                        pe.wait_ge(exp_done, nth(i, SUBS, k))
                    for g in range(GROUPS):
                        nc.tensor.matmul(st_ps[:, g, :], kst[par][:, g, k * SUB:k * SUB + P],
                                         qst[par][:, k, g * 512:(g + 1) * 512], start=True, stop=False)
                        last = nc.tensor.matmul(st_ps[:, g, :], ident_b[:, :], far[:, :, :].rearrange("p h q -> p (h q)"), start=False, stop=True)
                    last.then_inc(st_full, 1)
                if attend and kind == "PV":
                    if k == 0:
                        pe.wait_ge(v3_done, nth(i, 1, 1))
                    pe.wait_ge(pl_done, nth(i, SUBS, k + 1))
                    if not (isinstance(i, int) and i == 0 and k == 0):
                        pe.wait_ge(o_done, nth(i, SUBS, k))
                    for a in range(PAIRS):
                        v = v3[par][:, 2 * k + a // (PAIRS // 2), 0:VW]
                        nc.tensor.matmul(pv_ps[:, a * VW:(a + 1) * VW], prob_h[:, a * P:(a + 1) * P], v, start=True, stop=False)
                        last = nc.tensor.matmul(pv_ps[:, a * VW:(a + 1) * VW], prob_l[:, a * P:(a + 1) * P], v, start=False, stop=True)
                    last.then_inc(pv_full, 1)
                if attend and kind == "OT":
                    for s in range(2):
                        last = nc.tensor.transpose(misc[:, s * P:(s + 1) * P], o[:, (2 * k + s) % 4, :], ident[:, :])
                    last.then_inc(misc_full, 1)
                if attend and kind == "WO":
                    three(misc[:, 0:DIM], [(oT_h[:, r, :], oT_l[:, r, :], wo_h[:, r, :], wo_l[:, r, :]) for r in range(2)]).then_inc(misc_full, 1)
                if attend and kind == "X2T":
                    for c in range(KC):
                        last = nc.tensor.transpose(misc[:, c * P:(c + 1) * P], xn2[:, k % 2, c * P:(c + 1) * P], ident[:, :])
                    last.then_inc(misc_full, 1)
                if attend and kind == "LT":
                    n = 0
                    for c in range(KC):
                        for w in (wkv_h, wkv_l):
                            for x in (x2_h, x2_l):
                                last = nc.tensor.matmul(misc[:, :], w[:, c, :], x[par][:, c, :], start=(n == 0), stop=(n == 4 * KC - 1))
                                n += 1
                    last.then_inc(misc_full, 1)
                if attend and kind == "LG":
                    for t in range(TILES):
                        last = nc.tensor.transpose(misc[:, t * EXPERTS:(t + 1) * EXPERTS], lT[:, t * P:(t + 1) * P], ident[R0:R0 + EXPERTS, R0:R0 + EXPERTS])
                    last.then_inc(misc_full, 1)
                if kind == "M" and experts:
                    t, g = k // EG, k % EG
                    if k == 0 and isinstance(j, int) and j == 0:
                        pe.wait_ge(e_split, EXPERTS)
                    before = k - 2
                    if before >= 0 or not (isinstance(j, int) and j == 0):
                        tb, gb = before // EG, before % EG
                        if gb in BY_ACT:
                            pe.wait_ge(e_read_act, nth(j, TILES * len(BY_ACT), tb * len(BY_ACT) + BY_ACT.index(gb) + 1))
                        else:
                            pe.wait_ge(acc_seq, ACC_0 + nth(j, 2 * TILES * len(BY_DVE), 2 * (tb * len(BY_DVE) + BY_DVE.index(gb) + 1)))
                    rows = slice(t * P, (t + 1) * P)
                    three(e_ps[:, k % 2, :], [(x2_h[pj][:, c, rows], x2_l[pj][:, c, rows], we_h[:, c, 2 * g:2 * g + 2, :], we_l[:, c, 2 * g:2 * g + 2, :])
                                              for c in range(KC)]).then_inc(e_full, 1)

            program(pe, step)


R_STEPS = 16


def kernel(L0_attn_x, L0_attn_Wq, L0_attn_bq, L0_attn_Wk, L0_attn_bk, L0_attn_Wv, L0_attn_bv, L0_attn_Wo, L0_attn_bo,
           L0_ffn_router_w, L0_ffn_router_b, L0_ffn_expert_w):
    import numpy as np
    import concourse.bacc as bacc
    from concourse.bass_utils import run_bass_kernel_spmd

    x = np.pad(np.asarray(L0_attn_x), ((0, 0), (HALF, HALF), (0, 0)))
    x_halo = np.stack([x[b, s:s + HALO] for b in range(BATCH) for s in range(0, SEQ, BLOCK)])
    by_dim = (GROUPS, PER_GROUP, HD)
    wq = np.asarray(L0_attn_Wq).reshape(DIM, *by_dim).transpose(0, 1, 3, 2).reshape(DIM, DIM)
    bq = np.asarray(L0_attn_bq).reshape(by_dim).transpose(0, 2, 1).reshape(DIM)
    wo = np.asarray(L0_attn_Wo).reshape(PAIRS, 2, HD, DIM).transpose(1, 0, 2, 3).reshape(DIM, DIM)
    arrays = {
        "x_halo": x_halo, "wq": wq, "bq": bq, "wk": L0_attn_Wk, "bk": L0_attn_bk, "wv": L0_attn_Wv,
        "bv": L0_attn_bv, "wo": wo, "bo": L0_attn_bo, "rwt": np.asarray(L0_ffn_router_w).T,
        "rb": L0_ffn_router_b, "ew": L0_ffn_expert_w,
    }
    arrays = {k: np.ascontiguousarray(v) for k, v in arrays.items()}
    nc = bacc.Bacc("TRN2", target_bir_lowering=False, num_devices=1)
    args = [nc.dram_tensor(k, v.shape, mybir.dt.from_np(v.dtype), kind="ExternalInput").ap() for k, v in arrays.items()]
    out = nc.dram_tensor("out", (BLOCKS, BLOCK, DIM), F32, kind="ExternalOutput").ap()
    build(nc, *args, out)
    r = run_bass_kernel_spmd(nc, [arrays], core_ids=[0])
    return r.results[0]["out"].reshape(BATCH, SEQ, DIM)
```

```python
from contextlib import ExitStack

import concourse.bass as bass
from concourse import mybir

P = 128
DIM = 256
KC = DIM // P
HEADS = 16
GROUPS = 2
HD = DIM // HEADS
PER_GROUP = HEADS // GROUPS
WINDOW = 64
HALF = WINDOW // 2
BATCH, SEQ = 4, 1024
BLOCK = 512
HALO = BLOCK + 2 * HALF
BLOCKS = BATCH * SEQ // BLOCK
TILES = BLOCK // P
SUB = 64
SUBS = BLOCK // SUB
PAIRS = HEADS // 2
SLOTS_QK = 6
ROWS = SLOTS_QK * HD
MAXPARTS = 2
Q_PART = [0, 0, 0, 1, 1, 2]
K_PART = [0, 1, 2, 0, 1, 0]
VW = 3 * HD + 1
EXPERTS = 16
R0 = 2 * GROUPS * HD
TOP_K = 6
EPS_LN = 1e-5
EPS_GATE = 1e-10
FAR = -1e30
HUGE = 3e38
EG = EXPERTS // 2
QK_LOADS = 16 * SLOTS_QK * (GROUPS + 1)
BY_ACT = (1, 3, 5, 7)
BY_DVE = tuple(g for g in range(EG) if g not in BY_ACT)
STAGES = 4

ALU = mybir.AluOpType
ACT = mybir.ActivationFunctionType
AX = mybir.AxisListType
F32 = mybir.dt.float32
F32R = mybir.dt.float32r
BF16 = mybir.dt.bfloat16
F16 = mybir.dt.float16
U8 = mybir.dt.uint8

FRONT_ORDER = [("LN1", 0), ("T", 0), ("T", 1), ("T", 2), ("KV", 0), ("KV", 1), ("KVb", 0), ("VT", 0),
               ("VTb", 0), ("Q", 0), ("Qb", 0), ("KL", 0), ("Q", 1), ("Qb", 1), ("QL", 0), ("QL", 1)]
TAIL = [("OT", 3), ("WO", 3), ("XN", 3), ("X2T", 3), ("LT", 0), ("LG", 0)] + [("R", k) for k in range(7)]
SLOTS = [
    [("LN1", 0), ("M",)],
    [("S", 0), ("OT", 3), ("M",), ("MT", 0), ("M",), ("WO", 3)],
    [("S", 1), ("XN", 3), ("M",), ("T", 0), ("ST", 0), ("MT", 1), ("M",), ("T", 1)],
    [("S", 2), ("M",), ("T", 2), ("M",), ("ST", 1), ("MT", 2), ("M",), ("X2T", 3), ("PV", 0), ("M",), ("KV", 0), ("LT", 0)],
    [("S", 3), ("M",), ("KV", 1), ("M",), ("LG", 0), ("MT", 3), ("R", 0), ("ST", 2)],
    [("S", 4), ("KVb", 0), ("R", 1), ("PV", 1), ("M",), ("VT", 0), ("M",), ("R", 2), ("MT", 4), ("R", 3), ("VTb", 0),
     ("OT", 0), ("R", 4), ("R", 5), ("ST", 3), ("M",), ("PV", 2), ("Q", 0), ("M",), ("R", 6), ("WO", 0)],
    [("S", 5), ("ST", 4), ("KL", 0), ("Qb", 0), ("XN", 0), ("M",), ("Q", 1), ("M",), ("MT", 5), ("Qb", 1), ("PV", 3)],
    [("S", 6), ("M",), ("X2T", 0), ("M",)],
    [("S", 7), ("MT", 6), ("OT", 1), ("M",), ("ST", 5), ("M",), ("PV", 4), ("WO", 1), ("M",), ("MT", 7), ("ST", 6),
     ("QL", 0), ("QL", 1), ("M",), ("PV", 5), ("M",), ("XN", 1), ("X2T", 1), ("ST", 7), ("M",), ("OT", 2), ("M",),
     ("PV", 6), ("M",), ("WO", 2), ("M",), ("M",), ("XN", 2), ("PV", 7), ("X2T", 2), ("M",), ("M",), ("M",)],
]
ALL_GROUPS = TILES * EG
LAGGING = 15
ORDER, _m = [], 0
for _slot in SLOTS:
    for _tag in _slot:
        ORDER.append(_tag if _tag[0] != "M" else ("M", _m))
        _m += _tag[0] == "M"
assert _m == ALL_GROUPS, _m
IN_FRONT = {t[0] for t in FRONT_ORDER}
USES = ("MT", "T", "Q", "KV", "VT", "PV", "OT", "WO", "X2T", "LT", "LG")
FRONT_USES = [t for t in FRONT_ORDER if t[0] in USES]
STEP_USES = [t for t in ORDER if t[0] in USES]
assert len(STEP_USES) % 2 == 0
FIRST_USES = [t for t in STEP_USES if t not in TAIL]
TAIL_USES = [t for t in TAIL if t[0] in USES]
LAST_USES = [t for t in STEP_USES if t[0] not in IN_FRONT]


def nth(block, per, k):
    return block * per + k


P_STEPS = 5
R_STEPS = 16
R_ENDS = [2, 4, 6, 8, 10, 13]


def wait_some(e, sem, value):
    if not (isinstance(value, int) and value <= 0):
        e.wait_ge(sem, value)


def build(nc, x_halo, wq, bq, wk, bk, wv, bv, wo, bo, rwt, rb, ew, out):
    with ExitStack() as ctx:
        def sb(name, shape, dt):
            return ctx.enter_context(nc.sbuf_tensor(name, shape, dt))

        def ps(name, shape, dt=F32):
            return ctx.enter_context(nc.psum_tensor(name, shape, dt))

        def sem(name):
            return ctx.enter_context(nc.semaphore(name))

        q_dram = nc.dram_tensor("q_parts", [BLOCKS, GROUPS, 3, SUBS, P, SUB], BF16).ap()
        k_dram = nc.dram_tensor("k_parts", [BLOCKS, 3, GROUPS * HD, HALO], BF16).ap()

        s_ps = ps("s_ps", [P, PAIRS, P])
        st_ps = ps("st_ps", [P, GROUPS, 512])
        e_ps = ps("e_ps", [P, 2, 512])
        misc2 = ps("misc2", [P, 2, 512])

        stage = sb("stage", [P, STAGES, 512], F32)
        wq_h, wq_l = sb("wq_h", [P, KC, DIM], F32R), sb("wq_l", [P, KC, DIM], F32R)
        wkv_h, wkv_l = sb("wkv_h", [P, KC, P], F32R), sb("wkv_l", [P, KC, P], F32R)
        wo_h, wo_l = sb("wo_h", [P, 2, DIM], F32R), sb("wo_l", [P, 2, DIM], F32R)
        we_h = sb("we_h", [P, KC, EXPERTS, DIM], F32R)
        we_l = sb("we_l", [P, KC, EXPERTS, DIM], F32R)
        bq_c = sb("bq_c", [P, GROUPS], F32)
        bkv = sb("bkv", [1, 64], F32)
        bkv_h, bkv_l = sb("bkv_h", [1, P], F32R), sb("bkv_l", [1, P], F32R)
        bo_b = sb("bo_b", [P, DIM], F32)
        rb_c = sb("rb_c", [R0 + EXPERTS, 1], F32)
        valid = sb("valid", [1, HALO + HALF], F32R)
        ident = sb("ident", [P, P], F32)
        ident_b = sb("ident_b", [P, P], BF16)
        far = sb("far", [P, PER_GROUP, SUB], BF16)
        upper = sb("upper", [P, PAIRS, SUB], U8)
        expo = sb("expo", [P, 8], F32)
        eps = sb("eps", [P, 8], F32)
        xh = sb("xh", [P, TILES + 1, DIM], F32)
        st1 = sb("st1", [P, TILES + 1, 6], F32)
        mv1 = sb("mv1", [P, TILES + 1, 2], F32)
        ve1 = sb("ve1", [P, TILES + 1], F32)
        rstd1 = sb("rstd1", [P, TILES + 1], F32)
        xn = xh
        xT_h, xT_l = sb("xT_h", [P, KC, HALO], F32R), sb("xT_l", [P, KC, HALO], F32R)
        qp = sb("qp", [P, GROUPS, 3, BLOCK], BF16)
        rq = sb("rq", [P, GROUPS, BLOCK], F32)
        kp = sb("kp", [GROUPS * HD, 3, HALO], BF16)
        rq_flat = rq[:, :, :].rearrange("p g t -> p (g t)")
        rk = rq_flat[0:GROUPS * HD, 0:HALO]
        rv = rq_flat[:, HALO:HALO + SUBS * GROUPS * HD].rearrange("p (c d) -> p c d", d=HD)
        rows64 = sb("rows64", [R0 + EXPERTS, HALO], F32)
        vT = rows64
        lT = rows64[R0:R0 + EXPERTS, 0:BLOCK]
        qst = [sb(f"qst{p}", [ROWS + MAXPARTS, SUBS, HEADS * SUB], BF16) for p in range(2)]
        kst = [sb(f"kst{p}", [ROWS + MAXPARTS, GROUPS, HALO], BF16) for p in range(2)]
        v3 = [sb(f"v3{p}", [P, SUBS * GROUPS, VW + 1], BF16) for p in range(2)]
        negmax = sb("negmax", [P, 2, PAIRS], F32)
        mp = sb("mp", [PAIRS, 2, MAXPARTS, P], BF16)
        prob = sb("prob", [P, GROUPS * 512], F32)
        prob_h, prob_l = sb("prob_h", [P, GROUPS * 512], F16), sb("prob_l", [P, GROUPS * 512], F16)
        upper_f = prob[:, 0:PAIRS * SUB // 2].bitcast(BF16).rearrange("p (a q) -> p a q", a=PAIRS)
        osum = sb("osum", [P, PAIRS, HD], F32)
        rden = sb("rden", [P, PAIRS], F32)
        o = sb("o", [P, 4, PAIRS * HD], F32)
        oT_h, oT_l = sb("oT_h", [P, 2, P], F32R), sb("oT_l", [P, 2, P], F32R)
        x1 = [sb(f"x1{p}", [P, TILES, DIM], F32) for p in range(2)]
        st2 = sb("st2", [P, 2, 6], F32)
        mv2 = sb("mv2", [P, 2, 2], F32)
        ve2 = sb("ve2", [P, 2], F32)
        rstd2 = sb("rstd2", [P, 2], F32)
        xn2 = sb("xn2", [P, 2, DIM], F32)
        x2_h = [sb(f"x2_h{p}", [P, KC, BLOCK], F32R) for p in range(2)]
        x2_l = [sb(f"x2_l{p}", [P, KC, BLOCK], F32R) for p in range(2)]
        lg = sb("lg", [P, TILES, EXPERTS + 8], F32)
        m8 = sb("m8", [P, TILES, 8], F32)
        ld = sb("ld", [P, TILES, EXPERTS], F32)
        le = sb("le", [P, TILES, EXPERTS], F32)
        rep = sb("rep", [P, TILES, EXPERTS + 8], F32)
        sel = sb("sel", [P, TILES, EXPERTS], F32)
        z = sb("z", [P, 6, TILES], F32)
        gate = [sb(f"gate{p}", [P, TILES, EXPERTS], F32) for p in range(2)]
        etop = [sb(f"etop{p}", [P, TILES], F32) for p in range(2)]
        acc = sb("acc", [P, 2, 2, DIM], F32)
        tmp = stage[:, 0:2, :]
        acc_p = stage[:, 2, :]
        y = stage[:, 3, :].rearrange("p (a n) -> p a n", a=2)

        w_in = sem("w_in")
        b_in = sem("b_in")
        e_in = [sem(f"e_in{k}") for k in range(STAGES)]
        w_high = sem("w_high")
        w_split = sem("w_split")
        e_high = sem("e_high")
        e_split = sem("e_split")
        b_high = sem("b_high")
        zeroed = sem("zeroed")
        ones_up = sem("ones_up")
        masks_up = sem("masks_up")
        masks_ok = sem("masks_ok")
        x_in = sem("x_in")
        xres_in = sem("xres_in")
        ln1_stat, ln1_mv = sem("ln1_stat"), sem("ln1_mv")
        ln1_ve, ln1_rstd = sem("ln1_ve"), sem("ln1_rstd")
        xn_ready = sem("xn_ready")
        misc_full = sem("misc_full")
        misc_free = sem("misc_free")
        xT_high = sem("xT_high")
        q1_done, q2_done = sem("q1_done"), sem("q2_done")
        q3_done = sem("q3_done")
        q_out = [sem(f"q_out{g}") for g in range(GROUPS)]
        k1_done = sem("k1_done")
        k2_done = sem("k2_done")
        k3_done = sem("k3_done")
        k_out = sem("k_out")
        v1_done, v2_done = sem("v1_done"), sem("v2_done")
        v3_done = sem("v3_done")
        qk_in = sem("qk_in")
        s_full = sem("s_full")
        s_sel = sem("s_sel")
        max_done = sem("max_done")
        m1_done = sem("m1_done")
        m_in = [sem(f"m_in{p}") for p in range(2)]
        st_full = sem("st_full")
        exp_done = sem("exp_done")
        ph_done = sem("ph_done")
        pl_done = sem("pl_done")
        o_done = sem("o_done")
        oT_high = sem("oT_high")
        xb_ready = sem("xb_ready")
        ln2_stat, ln2_mv = sem("ln2_stat"), sem("ln2_mv")
        ln2_ve, ln2_rstd = sem("ln2_ve"), sem("ln2_rstd")
        xn2_ready = sem("xn2_ready")
        x2_high = sem("x2_high")
        r_seq = sem("r_seq")
        r_exp = sem("r_exp")
        gates_ready = sem("gates_ready")
        e_full = sem("e_full")
        e_read_act = sem("e_read_act")
        acc_seq = sem("acc_seq")
        p_seq = sem("p_seq")
        y_done = sem("y_done")
        passed_dve, passed_pe = sem("passed_dve"), sem("passed_pe")
        y_out = [sem(f"y_out{p}") for p in range(2)]

        def use_no(tag, i, first, front):
            if first:
                return FRONT_USES.index(tag)
            if tag in TAIL:
                i = i + 1
            if isinstance(i, int) and i == 0:
                return len(FRONT_USES) + FIRST_USES.index(tag)
            if isinstance(i, int) and i == BLOCKS:
                done = TAIL_USES.index(tag)
                return nth(i - 1, len(STEP_USES), len(FRONT_USES) - len(TAIL_USES)) + len(LAST_USES) + done
            uses = LAST_USES if isinstance(i, int) and i == BLOCKS - 1 else STEP_USES
            return nth(i, len(STEP_USES), len(FRONT_USES) - len(TAIL_USES) + uses.index(tag))

        def pv_before(i, k):
            return (use_no(("PV", k - 1), i, False, True) if k else use_no(("PV", SUBS - 1), i - 1, False, True)) + 1

        def bank(tag, i, first, front):
            if not isinstance(i, int):
                i = 1
            return misc2[:, use_no(tag, i, first, front) % 2, :]

        block = ctx.enter_context(nc.Block())

        def tile_before(k, j, pj, g):
            if k % EG != g or (isinstance(j, int) and j == 0 and k < EG):
                return None
            return (j, pj, k // EG - 1) if k >= EG else (j - 1, 1 - pj, TILES - 1)

        def program(e, step, lagging=LAGGING + 1):
            def one(i, par, front=True, attend=True, behind=2):
                for tag in ORDER:
                    if tag[0] == "M" and behind == 0:
                        step(("E", tag[1]), i, par, first=False, front=False, attend=False, experts=False)
                    elif tag[0] == "M":
                        lag = 2 if tag[1] < lagging else 1
                        if lag <= behind:
                            step(("M", (tag[1] - lagging) % ALL_GROUPS), i - lag + 1, (par + lag + 1) % 2,
                                 first=False, front=False, attend=False, experts=True)
                    elif tag in TAIL:
                        if behind:
                            step(tag, i - 1, 1 - par, first=False, front=False, attend=True, experts=False)
                    elif attend:
                        step(tag, i, par, first=False, front=front, attend=True, experts=False)

            for tag in FRONT_ORDER:
                step(tag, 0, 1, first=True, front=True, attend=False, experts=False)
            one(0, 0, behind=0)
            one(1, 1, behind=1)
            with e.Fori(1, BLOCKS // 2 - 1) as n:
                for half in range(2):
                    one(n * 2 + half, half)
            one(BLOCKS - 2, 0)
            one(BLOCKS - 1, 1, front=False)
            one(BLOCKS, 0, front=False, attend=False)
            for k in range(ALL_GROUPS - lagging, ALL_GROUPS):
                step(("M", k), BLOCKS, 0, first=False, front=False, attend=False, experts=True)
            step(("END", 0), BLOCKS, 0, first=False, front=False, attend=False, experts=True)

        @block.sync
        def _(sp):
            sp.dma_start(xh[:, 0:TILES, :], x_halo[0, 0:BLOCK, :].rearrange("(t p) d -> p t d", p=P)).then_inc(x_in, 16)
            sp.dma_start(xh[0:2 * HALF, TILES, :], x_halo[0, BLOCK:HALO, :]).then_inc(x_in, 16)
            sp.dma_start(stage[:, 0, :].rearrange("p (c n) -> p c n", c=KC),
                         wq.rearrange("(c p) n -> p c n", p=P)).then_inc(w_in, 16)
            kv = stage[:, 1, 0:KC * 64].rearrange("p (c n) -> p c n", c=KC)
            sp.dma_start(kv[:, :, 0:32], wk.rearrange("(c p) n -> p c n", p=P)).then_inc(w_in, 16)
            sp.dma_start(kv[:, :, 32:64], wv.rearrange("(c p) n -> p c n", p=P)).then_inc(w_in, 16)
            sp.dma_start(stage[:, 2, :].rearrange("p (c n) -> p c n", c=2), wo.rearrange("(c p) n -> p c n", p=P)).then_inc(w_in, 16)
            sp.dma_start(stage[:, 3, 0:KC * EXPERTS].rearrange("p (c n) -> p c n", c=KC),
                         rwt.rearrange("(c p) n -> p c n", p=P)).then_inc(w_in, 16)
            for g in range(GROUPS):
                sp.dma_start(bq_c[:, g:g + 1], bq.rearrange("(n a) -> n a", a=1)[g * P:(g + 1) * P, :]).then_inc(b_in, 16)
            sp.dma_start(bkv[:, 0:32], bk.rearrange("(a n) -> a n", a=1)).then_inc(b_in, 16)
            sp.dma_start(bkv[:, 32:64], bv.rearrange("(a n) -> a n", a=1)).then_inc(b_in, 16)
            sp.dma_start(bo_b[:, :], bo.rearrange("(a n) -> a n", a=1).broadcast_to([P, DIM])).then_inc(b_in, 16)
            sp.dma_start(rb_c[R0:R0 + EXPERTS, :], rb.rearrange("(n a) -> n a", a=1)).then_inc(b_in, 16)

            def step(tag, i, par, first, front, attend, experts):
                kind, k = tag
                mb = bank(tag, i, first, front) if kind in USES and (front if kind in IN_FRONT else attend) else None
                f = 0 if first else i + 1
                pf = 0 if first else 1 - par
                if front and tag == ("T", 2):
                    g = f + 1
                    sp.wait_ge(misc_free, use_no(tag, i, first, front) + 1)
                    sp.dma_start(xh[:, 0:TILES, :], x_halo[g, 0:BLOCK, :].rearrange("(t p) d -> p t d", p=P)).then_inc(x_in, 16)
                    sp.dma_start(xh[0:2 * HALF, TILES, :], x_halo[g, BLOCK:HALO, :]).then_inc(x_in, 16)
                if attend and kind == "S" and k == 3:
                    if not (isinstance(i, int) and i < 2):
                        sp.wait_ge(acc_seq, nth(i - 2, 2 * TILES * len(BY_DVE), 2 * (TILES - 1) * len(BY_DVE) + 1))
                    sp.dma_start(x1[par][:, :, :], x_halo[i, HALF:HALF + BLOCK, :].rearrange("(t p) d -> p t d", p=P)).then_inc(xres_in, 16)
                if attend and kind == "MT":
                    sp.wait_ge(misc_free, use_no(tag, i, first, front) + 1)
                    for part in range(MAXPARTS):
                        sp.dma_start(qst[par][ROWS + part:ROWS + part + 1, k, :], mp[:, k % 2, part, :]).then_inc(m_in[k % 2], 16)
                if front and kind == "Qb":
                    sp.wait_ge(q3_done, nth(f, 2, k + 1))
                    sp.dma_start(q_dram[f, k].rearrange("s u p q -> p (s u) q"),
                                 qp[:, k, :, :].rearrange("p s (u q) -> p (s u) q", q=SUB)).then_inc(q_out[k], 16)
                if front and kind == "QL":
                    sp.wait_ge(q_out[k], nth(f, 16, 16))
                    for s in range(SLOTS_QK):
                        sp.dma_start(qst[pf][s * HD:(s + 1) * HD, :, k * 512:(k + 1) * 512],
                                     q_dram[f, k, Q_PART[s]].rearrange("u (d h) q -> d u (h q)", d=HD)).then_inc(qk_in, 16)
                if front and kind == "KVb":
                    sp.wait_ge(k3_done, nth(f, 1, 1))
                    sp.dma_start(k_dram[f].rearrange("s p t -> p s t"), kp[:, :, :]).then_inc(k_out, 16)
                if front and kind == "KL":
                    sp.wait_ge(k_out, nth(f, 16, 16))
                    for s in range(SLOTS_QK):
                        sp.dma_start(kst[pf][s * HD:(s + 1) * HD, :, :],
                                     k_dram[f, K_PART[s], :, :].rearrange("(g d) t -> d g t", d=HD)).then_inc(qk_in, 16)
                if kind == "E" and k % 2 == 0:
                    if k == 0:
                        sp.wait_ge(w_split, 4)
                    for ex in range(STAGES) if k == 0 else range(k // 2 + STAGES - 1, min(k // 2 + STAGES, EXPERTS)):
                        if k > 0:
                            sp.wait_ge(e_split, ex - STAGES + 1)
                        sp.dma_start(stage[:, ex % STAGES, :].rearrange("p (c n) -> p c n", c=KC),
                                     ew[ex].rearrange("(c p) n -> p c n", p=P)).then_inc(e_in[ex % STAGES], 16)

                late = (BLOCKS - 1, 1, TILES - 1) if kind == "END" else tile_before(k, i - 1, 1 - par, 4) if kind == "M" else None
                if late:
                    j, _, t = late
                    sp.wait_ge(y_done, nth(j, TILES, t + 1))
                    sp.dma_start(out[j, t * P:(t + 1) * P, :], y[:, t % 2, :]).then_inc(y_out[t % 2], 16)

            program(sp, step)
            for p in range(2):
                sp.wait_ge(y_out[p], 16 * BLOCKS * TILES // 2)

        @block.gpsimd
        def _(pool):
            nc.gpsimd.memset(ident[:, :], 0.0).then_inc(ones_up, 1)
            nc.gpsimd.memset(ident_b[:, :], 0.0).then_inc(ones_up, 1)
            nc.gpsimd.memset(far[:, :, :], 0.0).then_inc(ones_up, 1)
            nc.gpsimd.memset(upper_f[:, :, :], 1.0).then_inc(ones_up, 1)
            nc.gpsimd.memset(expo[:, :], -0.5).then_inc(ones_up, 1)
            nc.gpsimd.memset(eps[:, :], EPS_LN).then_inc(ones_up, 1)
            pool.wait_ge(ones_up, 6)
            for t in (ident, ident_b):
                nc.gpsimd.affine_select(out=t[:, :], in_=t[:, :], compare_op=ALU.not_equal, fill=1.0, base=0,
                                        pattern=[[-1, P]], channel_multiplier=1).then_inc(masks_up, 1)
            nc.gpsimd.affine_select(out=far[:, :, :], in_=far[:, :, :], compare_op=ALU.is_ge, fill=FAR, base=0,
                                    pattern=[[0, PER_GROUP], [-1, SUB]], channel_multiplier=1).then_inc(masks_up, 1)
            pool.wait_ge(masks_up, 3)
            nc.gpsimd.affine_select(out=far[:, :, :], in_=far[:, :, :], compare_op=ALU.is_ge, fill=FAR, base=WINDOW - 1,
                                    pattern=[[0, PER_GROUP], [1, SUB]], channel_multiplier=-1).then_inc(masks_up, 1)
            for r in range(2):
                pool.wait_ge(masks_up, 4 + r)
                part = upper_f[r * SUB:(r + 1) * SUB, :, :]
                nc.gpsimd.affine_select(out=part, in_=part, compare_op=ALU.is_gt, fill=0.0, base=0,
                                        pattern=[[0, PAIRS], [-1, SUB]], channel_multiplier=1).then_inc(masks_up, 1)
            pool.wait_ge(masks_up, 6)

            def step(tag, i, par, first, front, attend, experts):
                kind, k = tag
                mb = bank(tag, i, first, front) if kind in USES and (front if kind in IN_FRONT else attend) else None
                f = 0 if first else i + 1
                pf = 0 if first else 1 - par
                j, pj = i - 1, 1 - par
                if front and kind == "LN1":
                    pool.wait_ge(ln1_mv, nth(f, 1, 1))
                    nc.gpsimd.tensor_tensor(ve1[:, :], mv1[:, :, 1], eps[:, 0:TILES + 1], ALU.add).then_inc(ln1_ve, 1)
                    pool.wait_ge(ln1_ve, nth(f, 1, 1))
                    nc.gpsimd.tensor_tensor(rstd1[:, :], ve1[:, :], expo[:, 0:TILES + 1], ALU.pow).then_inc(ln1_rstd, 1)
                if attend and tag == ("PV", 1):
                    pool.wait_ge(xres_in, nth(i, 16, 16))
                    if isinstance(i, int) and i == 0:
                        pool.wait_ge(b_in, 16 * 6)
                    nc.gpsimd.tensor_tensor(x1[par][:, :, :], x1[par][:, :, :], bo_b[:, :].rearrange("p (a n) -> p a n", a=1).broadcast_to([P, TILES, DIM]),
                                            ALU.add).then_inc(xb_ready, 1)
                if attend and (tag == ("ST", 0) or kind == "PV" and k < SUBS - 1):
                    k = 0 if kind == "ST" else k + 1
                    pool.wait_ge(ph_done, nth(i, SUBS, k + 1))
                    nc.gpsimd.tensor_tensor(prob_l[:, :], prob[:, :], prob_h[:, :], ALU.subtract).then_inc(pl_done, 1)
                if attend and kind == "WO":
                    pool.wait_ge(ln2_mv, nth(i, TILES, k + 1))
                    nc.gpsimd.tensor_tensor(ve2[:, k % 2:k % 2 + 1], mv2[:, k % 2, 1:2], eps[:, 0:1], ALU.add).then_inc(ln2_ve, 1)
                    pool.wait_ge(ln2_ve, nth(i, TILES, k + 1))
                    nc.gpsimd.tensor_tensor(rstd2[:, k % 2:k % 2 + 1], ve2[:, k % 2:k % 2 + 1], expo[:, 0:1], ALU.pow).then_inc(ln2_rstd, 1)
                if front and kind == "Qb":
                    pool.wait_ge(q2_done, nth(f, 2, k + 1))
                    nc.gpsimd.tensor_tensor(qp[:, k, 2, :], rq[:, k, :], qp[:, k, 1, :], ALU.subtract).then_inc(q3_done, 1)
                if front and kind == "KVb":
                    pool.wait_ge(k2_done, nth(f, 1, 1))
                    nc.gpsimd.tensor_tensor(kp[:, 2, :], rk[:, :], kp[:, 1, :], ALU.subtract).then_inc(k3_done, 1)
                if front and kind == "VTb":
                    pool.wait_ge(v2_done, nth(f, 1, 1))
                    nc.gpsimd.tensor_tensor(v3[pf][:, :, 2 * HD:3 * HD], rv[:, :, :], v3[pf][:, :, HD:2 * HD],
                                            ALU.subtract).then_inc(v3_done, 1)
                late = (BLOCKS - 1, 1, TILES - 1) if kind == "END" else tile_before(k, j, pj, 1) if kind == "M" else None
                if late:
                    lj, _, t = late
                    pool.wait_ge(p_seq, nth(lj, P_STEPS * TILES, P_STEPS * t + 3))
                    wait_some(pool, y_out[t % 2], nth(lj, 16 * TILES // 2, 16 * (t // 2)))
                    nc.gpsimd.tensor_tensor(y[:, t % 2, :], acc_p[:, 0:DIM], acc_p[:, DIM:2 * DIM], ALU.add).then_inc(p_seq, 1)
                    pool.wait_ge(acc_seq, nth(lj, 2 * TILES * len(BY_DVE), 2 * (t + 1) * len(BY_DVE)))
                    for q in range(2):
                        pool.wait_ge(p_seq, nth(lj, P_STEPS * TILES, P_STEPS * t + 4 + q))
                        nc.gpsimd.tensor_tensor(y[:, t % 2, :], y[:, t % 2, :], acc[:, t % 2, q, :], ALU.add).then_inc((p_seq, y_done)[q], 1)
                if kind == "M" and k % EG in BY_ACT[1:]:
                    t, a = k // EG, BY_ACT.index(k % EG)
                    pool.wait_ge(e_read_act, nth(j, TILES * len(BY_ACT), t * len(BY_ACT) + a + 1))
                    wait_some(pool, p_seq, nth(j, P_STEPS * TILES, P_STEPS * t + (a - 1 if a > 1 else 4 - P_STEPS)))
                    nc.gpsimd.tensor_tensor(acc_p[:, :], tmp[:, 0, :] if a == 1 else acc_p[:, :], tmp[:, a % 2, :], ALU.add).then_inc(p_seq, 1)

            program(pool, step)

        @block.scalar
        def _(act):
            act.wait_ge(w_in, 16 * 5)
            act.wait_ge(zeroed, 1)
            for dst, src in ((wq_h[:, :, :], stage[:, 0, :].rearrange("p (c n) -> p c n", c=KC)),
                             (wkv_h[:, :, 0:64], stage[:, 1, 0:KC * 64].rearrange("p (c n) -> p c n", c=KC)),
                             (wo_h[:, :, :], stage[:, 2, :].rearrange("p (c n) -> p c n", c=2)),
                             (wkv_h[:, :, R0:R0 + EXPERTS], stage[:, 3, 0:KC * EXPERTS].rearrange("p (c n) -> p c n", c=KC))):
                nc.scalar.activation(dst, src, ACT.Copy).then_inc(w_high, 1)
            act.wait_ge(b_in, 16 * 6)
            nc.scalar.activation(bkv_h[:, 0:64], bkv[:, :], ACT.Copy).then_inc(b_high, 1)

            def step(tag, i, par, first, front, attend, experts):
                kind, k = tag
                mb = bank(tag, i, first, front) if kind in USES and (front if kind in IN_FRONT else attend) else None
                f = 0 if first else i + 1
                pf = 0 if first else 1 - par
                j, pj = i - 1, 1 - par
                if kind in USES and (front if kind in IN_FRONT else attend):
                    act_waits_misc = kind not in ("MT", "PV", "WO", "LT", "LG")
                    if act_waits_misc:
                        act.wait_ge(misc_full, use_no(tag, i, first, front) + 1)
                if front and kind == "T":
                    if k < KC:
                        nc.scalar.activation(xT_h[:, k, 0:BLOCK], mb[:, :], ACT.Copy).then_inc(xT_high, 1)
                    else:
                        nc.scalar.activation(xT_h[:, :, BLOCK:HALO],
                                             mb[:, 0:KC * 2 * HALF].rearrange("p (c n) -> p c n", c=KC), ACT.Copy).then_inc(xT_high, 1)
                if front and kind == "Q":
                    if not first:
                        act.wait_ge(q_out[k], nth(f, 16, 0))
                    nc.scalar.activation(qp[:, k, 0, :], mb[:, :], ACT.Identity, bias=bq_c[:, k:k + 1]).then_inc(q1_done, 1)
                    act.wait_ge(misc_free, use_no(tag, i, first, front) + 1)
                    nc.scalar.activation(qp[:, k, 1, :], rq[:, k, :], ACT.Copy).then_inc(q2_done, 1)
                if front and kind == "KV":
                    h = HALO // 2
                    if not first:
                        act.wait_ge(k_out, nth(f, 16, 0))
                    nc.scalar.activation(kp[:, 0, k * h:(k + 1) * h], mb[0:32, 0:h], ACT.Copy)
                    nc.scalar.activation(vT[32:64, k * h:(k + 1) * h], mb[32:64, 0:h], ACT.Copy).then_inc(k1_done, 1)
                    if k == 1:
                        act.wait_ge(misc_free, use_no(tag, i, first, front) + 1)
                        nc.scalar.activation(kp[:, 1, :], rk[:, :], ACT.Copy).then_inc(k2_done, 1)
                if front and kind == "VT":
                    nc.scalar.activation(v3[pf][:, :, 0:HD], mb[:, 0:SUBS * 32].rearrange("p (c d) -> p c d", d=HD),
                                         ACT.Copy).then_inc(v1_done, 1)
                    act.wait_ge(misc_free, use_no(tag, i, first, front) + 1)
                    nc.scalar.activation(v3[pf][:, :, HD:2 * HD], rv[:, :, :], ACT.Copy).then_inc(v2_done, 1)
                if attend and kind == "ST":
                    act.wait_ge(st_full, nth(i, SUBS, k + 1))
                    if not (isinstance(i, int) and i == 0 and k == 0):
                        act.wait_ge(pl_done, nth(i, SUBS, k))
                    nc.scalar.activation(prob[:, :], st_ps[:, :, :].rearrange("p g n -> p (g n)"), ACT.Exp).then_inc(exp_done, 1)
                if attend and (tag == ("ST", 0) or kind == "PV" and k < SUBS - 1):
                    n = 0 if kind == "ST" else k + 1
                    act.wait_ge(exp_done, nth(i, SUBS, n + 1))
                    if not (isinstance(i, int) and i == 0 and n == 0):
                        act.wait_ge(misc_full, pv_before(i, n))
                    nc.scalar.activation(prob_h[:, :], prob[:, :], ACT.Copy).then_inc(ph_done, 1)
                if attend and kind == "OT":
                    nc.scalar.activation(oT_h[:, :, :].rearrange("p r (s q) -> p s r q", s=2),
                                         mb[:, 0:2 * P].rearrange("p (s r q) -> p s r q", s=2, r=2), ACT.Copy).then_inc(oT_high, 1)
                if attend and kind == "X2T":
                    nc.scalar.activation(x2_h[par][:, :, k * P:(k + 1) * P], mb[:, 0:KC * P].rearrange("p (c n) -> p c n", c=KC),
                                         ACT.Copy).then_inc(x2_high, 1)
                if attend and tag == ("R", 1):
                    act.wait_ge(r_seq, nth(i, R_STEPS, 2))
                    nc.scalar.activation(le[:, :, :], ld[:, :, :], ACT.Exp).then_inc(r_exp, 1)
                if kind == "M":
                    t, g = k // EG, k % EG
                    if g in BY_ACT:
                        a = BY_ACT.index(g)
                        act.wait_ge(e_full, nth(j, TILES * EG, k + 1))
                        act.wait_ge(gates_ready, nth(j, 1, 1))
                        wait_some(act, p_seq, nth(j, P_STEPS * TILES, P_STEPS * t + (1, 1, 2 - P_STEPS, 3 - P_STEPS)[a - 2]))
                        for q in range(2):
                            scale = gate[pj][:, t, 2 * g + q:2 * g + q + 1]
                            src, dst = e_ps[:, k % 2, q * DIM:(q + 1) * DIM], tmp[:, a % 2, q * DIM:(q + 1) * DIM]
                            if a == 0 and q == 0:
                                last = nc.scalar.activation(dst, src, ACT.Identity, scale=scale, bias=etop[pj][:, t:t + 1])
                            else:
                                last = nc.scalar.activation(dst, src, ACT.Copy, scale=scale)
                        last.then_inc(e_read_act, 1)
                if kind == "E" and k % 2 == 1:
                    ex = k // 2
                    act.wait_ge(e_in[ex % STAGES], 16 * (ex // STAGES + 1))
                    nc.scalar.activation(we_h[:, :, ex, :], stage[:, ex % STAGES, :].rearrange("p (c n) -> p c n", c=KC),
                                         ACT.Copy).then_inc(e_high, 1)

            program(act, step)

        @block.vector
        def _(dve):
            nc.vector.memset(xh[2 * HALF:P, TILES, :], 0.0)
            nc.vector.memset(lg[:, :, EXPERTS:], -HUGE)
            for t in (wkv_h, wkv_l):
                nc.vector.memset(t[:, :, :].bitcast(F32), 0.0)
            nc.vector.memset(bkv_h[:, :].bitcast(F32), 0.0)
            nc.vector.memset(bkv_l[:, :].bitcast(F32), 0.0).then_inc(zeroed, 1)
            nc.vector.memset(valid[:, :].bitcast(F32), 1.0).then_inc(zeroed, 1)
            dve.wait_ge(zeroed, 2)
            nc.vector.memset(valid[:, 0:HALF].bitcast(F32), 0.0)
            nc.vector.memset(valid[:, HALO:HALO + HALF].bitcast(F32), 0.0).then_inc(zeroed, 1)
            def split_weights():
                for n, (dst, src, high) in enumerate((
                        (wq_l[:, :, :], stage[:, 0, :].rearrange("p (c n) -> p c n", c=KC), wq_h[:, :, :]),
                        (wkv_l[:, :, 0:64], stage[:, 1, 0:KC * 64].rearrange("p (c n) -> p c n", c=KC), wkv_h[:, :, 0:64]),
                        (wo_l[:, :, :], stage[:, 2, :].rearrange("p (c n) -> p c n", c=2), wo_h[:, :, :]),
                        (wkv_l[:, :, R0:R0 + EXPERTS], stage[:, 3, 0:KC * EXPERTS].rearrange("p (c n) -> p c n", c=KC), wkv_h[:, :, R0:R0 + EXPERTS]))):
                    dve.wait_ge(w_high, n + 1)
                    nc.vector.tensor_tensor(dst, src, high.bitcast(F32), ALU.subtract).then_inc(w_split, 1)
                dve.wait_ge(b_high, 1)
                nc.vector.tensor_tensor(bkv_l[:, 0:64], bkv[:, :], bkv_h[:, 0:64].bitcast(F32), ALU.subtract).then_inc(b_high, 1)
                dve.wait_ge(masks_up, 6)
                nc.vector.tensor_copy(upper[:, :, :], upper_f[:, :, :]).then_inc(masks_ok, 1)
                dve.wait_ge(masks_ok, 1)

            def settled():
                dve.sem_inc(passed_dve, 1)

            def ln1(f):
                dve.wait_ge(x_in, nth(f, 32, 32))
                for n in range(TILES + 1):
                    last = nc.vector.bn_stats(st1[:, n, :], xh[:, n, :])
                last.then_inc(ln1_stat, 1)
                dve.wait_ge(ln1_stat, nth(f, 1, 1))
                settled()
                for n in range(TILES + 1):
                    last = nc.vector.bn_aggr(mv1[:, n, :], st1[:, n, :])
                last.then_inc(ln1_mv, 1)
                dve.wait_ge(ln1_rstd, nth(f, 1, 1))
                for n in range(TILES + 1):
                    last = nc.vector.tensor_scalar(xn[:, n, :], xh[:, n, :], mv1[:, n, 0:1], rstd1[:, n:n + 1],
                                                   ALU.subtract, ALU.mult)
                last.then_inc(xn_ready, 1)

            def router(i, par, part):
                def link(n, ins):
                    ins.then_inc(r_seq, 1)
                    if n < R_STEPS and n not in R_ENDS:
                        dve.wait_ge(r_seq, nth(i, R_STEPS, n))

                def wide(v):
                    return v.broadcast_to([P, TILES, EXPERTS])

                def z_(n):
                    return z[:, n, :].rearrange("p (t a) -> p t a", a=1)

                if part == 0:
                    dve.wait_ge(misc_free, use_no(("LG", 0), i, False, False) + 1)
                    settled()
                    for t in range(TILES):
                        last = nc.vector.max(m8[:, t, :], lg[:, t, 0:EXPERTS])
                    link(1, last)
                    link(2, nc.vector.tensor_tensor(ld[:, :, :], lg[:, :, 0:EXPERTS], wide(m8[:, :, 0:1]), ALU.subtract))
                else:
                    dve.wait_ge(r_seq, nth(i, R_STEPS, R_ENDS[part - 1]))
                if part == 1:
                    link(3, nc.vector.memset(m8[:, :, TOP_K:8], -HUGE))
                    settled()
                    for t in range(TILES):
                        last = nc.vector.match_replace(rep[:, t, :], m8[:, t, :], lg[:, t, :], HUGE)
                    link(4, last)
                if part == 2:
                    link(5, nc.vector.tensor_scalar(sel[:, :, :], rep[:, :, 0:EXPERTS], HUGE, None, ALU.is_equal))
                    dve.wait_ge(r_exp, nth(i, 1, 1))
                    link(6, nc.vector.tensor_reduce(z[:, 1, :], le[:, :, :], AX.X, ALU.add))
                if part == 3:
                    link(7, nc.vector.reciprocal(z[:, 2, :], z[:, 1, :]))
                    link(8, nc.vector.tensor_tensor(ld[:, :, :], le[:, :, :], wide(z_(2)), ALU.mult))
                if part == 4:
                    link(9, nc.vector.tensor_tensor(sel[:, :, :], sel[:, :, :], ld[:, :, :], ALU.mult))
                    link(10, nc.vector.tensor_reduce(z[:, 3, :], sel[:, :, :], AX.X, ALU.add))
                if part == 5:
                    link(11, nc.vector.tensor_scalar(z[:, 4, :], z[:, 3, :], EPS_GATE, None, ALU.add))
                    link(12, nc.vector.reciprocal(z[:, 5, :], z[:, 4, :]))
                    link(13, nc.vector.tensor_tensor(gate[par][:, :, :], sel[:, :, :], wide(z_(5)), ALU.mult))
                if part == 6:
                    link(14, nc.vector.tensor_reduce(z[:, 0, :], gate[par][:, :, :], AX.X, ALU.add))
                    nc.vector.tensor_scalar(etop[par][:, :], z[:, 0, :], EPS_GATE, None, ALU.mult)
                    link(15, nc.vector.tensor_scalar(z[:, 1, :], z[:, 0, :], EPS_GATE, None, ALU.max))
                    dve.wait_ge(r_seq, nth(i, R_STEPS, 15))
                    link(16, nc.vector.reciprocal(z[:, 2, :], z[:, 1, :]))
                    dve.wait_ge(r_seq, nth(i, R_STEPS, 16))
                    nc.vector.tensor_tensor(gate[par][:, :, :], gate[par][:, :, :], wide(z_(2)), ALU.mult).then_inc(gates_ready, 1)

            def step(tag, i, par, first, front, attend, experts):
                kind, k = tag
                mb = bank(tag, i, first, front) if kind in USES and (front if kind in IN_FRONT else attend) else None
                f = 0 if first else i + 1
                pf = 0 if first else 1 - par
                j, pj = i - 1, 1 - par
                use = use_no(tag, i, first, front) if kind in USES and (front if kind in IN_FRONT else attend) else None
                if front and kind == "LN1":
                    ln1(f)
                    if first:
                        split_weights()
                if first and kind == "KVb":
                    for p in range(2):
                        nc.vector.memset(kst[p][ROWS:ROWS + MAXPARTS, :, :], 1.0)
                        nc.vector.memset(v3[p][:, :, 3 * HD:VW + 1], 1.0)
                if front and kind == "T":
                    dve.wait_ge(misc_full, use + 1)
                    dve.wait_ge(xT_high, nth(f, 3, k + 1))
                    if k < KC:
                        d, s, h = xT_l[:, k, 0:BLOCK], mb[:, :], xT_h[:, k, 0:BLOCK]
                    else:
                        d, h = xT_l[:, :, BLOCK:HALO], xT_h[:, :, BLOCK:HALO]
                        s = mb[:, 0:KC * 2 * HALF].rearrange("p (c n) -> p c n", c=KC)
                    nc.vector.tensor_tensor(d, s, h.bitcast(F32), ALU.subtract).then_inc(misc_free, 1)
                if front and kind == "Q":
                    dve.wait_ge(misc_full, use + 1)
                    dve.wait_ge(q1_done, nth(f, 2, k + 1))
                    dve.wait_ge(k3_done, nth(f, 1, 1))
                    dve.wait_ge(v3_done, nth(f, 1, 1))
                    nc.vector.scalar_tensor_tensor(out=rq[:, k, :], in0=mb[:, :], scalar=bq_c[:, k:k + 1],
                                                   in1=qp[:, k, 0, :], op0=ALU.add, op1=ALU.subtract).then_inc(misc_free, 1)
                if front and kind == "KV":
                    h = HALO // 2
                    dve.wait_ge(misc_full, use + 1)
                    dve.wait_ge(k1_done, nth(f, 2, k + 1))
                    if not first:
                        dve.wait_ge(q3_done, nth(f, 2, 0))
                    nc.vector.tensor_tensor(rk[:, k * h:(k + 1) * h], mb[0:32, 0:h], kp[:, 0, k * h:(k + 1) * h],
                                            ALU.subtract).then_inc(misc_free, 1)
                if front and kind == "VT":
                    dve.wait_ge(misc_full, use + 1)
                    dve.wait_ge(v1_done, nth(f, 1, 1))
                    nc.vector.tensor_tensor(rv[:, :, :], mb[:, 0:SUBS * 32].rearrange("p (c d) -> p c d", d=HD),
                                            v3[pf][:, :, 0:HD], ALU.subtract).then_inc(misc_free, 1)
                if attend and kind == "S":
                    dve.wait_ge(s_full, nth(i, SUBS, k + 1))
                    settled()
                    nc.vector.copy_predicated(s_ps[:, :, 0:SUB], upper[:, :, :], s_ps[:, :, SUB:2 * SUB]).then_inc(s_sel, 1)
                    dve.wait_ge(s_sel, nth(i, SUBS, k + 1))
                    nc.vector.tensor_reduce(negmax[:, k % 2, :], s_ps[:, :, 0:SUB], AX.X, ALU.max, negate=True).then_inc(max_done, 1)
                if attend and kind == "MT":
                    dve.wait_ge(misc_full, use + 1)
                    if not (isinstance(i, int) and i == 0 and k < 2):
                        dve.wait_ge(m_in[k % 2], nth(i, 32 * SUBS // 2, 32 * (k // 2)))
                    nc.vector.tensor_copy(mp[:, k % 2, 0, :], mb[0:PAIRS, 0:P]).then_inc(m1_done, 1)
                    dve.wait_ge(m1_done, nth(i, SUBS, k + 1))
                    nc.vector.tensor_tensor(mp[:, k % 2, 1, :], mb[0:PAIRS, 0:P], mp[:, k % 2, 0, :], ALU.subtract).then_inc(misc_free, 1)
                if attend and kind == "PV":
                    dve.wait_ge(misc_full, use + 1)
                    part = mb[:, 0:PAIRS * VW].rearrange("p (a w) -> p a w", w=VW)
                    nc.vector.tensor_reduce(osum[:, :, :], part[:, :, 0:3 * HD].rearrange("p a (s d) -> p a d s", s=3),
                                            AX.X, ALU.add)
                    nc.vector.reciprocal(rden[:, :], part[:, :, 3 * HD]).then_inc(misc_free, 1)
                    dve.wait_ge(misc_free, use + 1)
                    nc.vector.tensor_tensor(o[:, k % 4, :].rearrange("p (a d) -> p a d", d=HD), osum[:, :, :],
                                            rden[:, :].rearrange("p (a d) -> p a d", d=1).broadcast_to([P, PAIRS, HD]), ALU.mult).then_inc(o_done, 1)
                if attend and kind == "OT":
                    dve.wait_ge(misc_full, use + 1)
                    dve.wait_ge(oT_high, nth(i, TILES, k + 1))
                    nc.vector.tensor_tensor(oT_l[:, :, :].rearrange("p r (s q) -> p s r q", s=2),
                                            mb[:, 0:2 * P].rearrange("p (s r q) -> p s r q", s=2, r=2),
                                            oT_h[:, :, :].bitcast(F32).rearrange("p r (s q) -> p s r q", s=2), ALU.subtract).then_inc(misc_free, 1)
                if attend and kind == "WO":
                    dve.wait_ge(misc_full, use + 1)
                    dve.wait_ge(xb_ready, nth(i, 1, 1))
                    nc.vector.tensor_tensor(x1[par][:, k, :], mb[:, 0:DIM], x1[par][:, k, :], ALU.add).then_inc(misc_free, 1)
                    dve.wait_ge(misc_free, use + 1)
                    nc.vector.bn_stats(st2[:, k % 2, :], x1[par][:, k, :]).then_inc(ln2_stat, 1)
                    dve.wait_ge(ln2_stat, nth(i, TILES, k + 1))
                    settled()
                    nc.vector.bn_aggr(mv2[:, k % 2, :], st2[:, k % 2, :]).then_inc(ln2_mv, 1)
                if attend and kind == "XN":
                    dve.wait_ge(ln2_rstd, nth(i, TILES, k + 1))
                    nc.vector.tensor_scalar(xn2[:, k % 2, :], x1[par][:, k, :], mv2[:, k % 2, 0:1], rstd2[:, k % 2:k % 2 + 1],
                                            ALU.subtract, ALU.mult).then_inc(xn2_ready, 1)
                if attend and kind == "X2T":
                    dve.wait_ge(misc_full, use + 1)
                    dve.wait_ge(x2_high, nth(i, TILES, k + 1))
                    nc.vector.tensor_tensor(x2_l[par][:, :, k * P:(k + 1) * P], mb[:, 0:KC * P].rearrange("p (c n) -> p c n", c=KC),
                                            x2_h[par][:, :, k * P:(k + 1) * P].bitcast(F32), ALU.subtract).then_inc(misc_free, 1)
                if attend and kind == "LT":
                    dve.wait_ge(misc_full, use + 1)
                    nc.vector.tensor_scalar(lT[:, :], mb[R0:R0 + EXPERTS, :], rb_c[R0:R0 + EXPERTS, 0:1], None, ALU.add).then_inc(misc_free, 1)
                if attend and kind == "LG":
                    dve.wait_ge(misc_full, use + 1)
                    nc.vector.tensor_copy(lg[:, :, 0:EXPERTS], mb[:, 0:TILES * EXPERTS].rearrange("p (t n) -> p t n", n=EXPERTS)).then_inc(misc_free, 1)
                if attend and kind == "R":
                    router(i, par, k)
                if kind == "M":
                    t, g = k // EG, k % EG
                    if g in BY_DVE:
                        a = BY_DVE.index(g)
                        dve.wait_ge(e_full, nth(j, TILES * EG, k + 1))
                        if k == 0:
                            dve.wait_ge(gates_ready, nth(j, 1, 1))
                        for q in range(2):
                            scale = gate[pj][:, t, 2 * g + q:2 * g + q + 1]
                            src = e_ps[:, k % 2, q * DIM:(q + 1) * DIM]
                            dst = acc[:, t % 2, q, :]
                            done = 2 * (t * len(BY_DVE) + a) + q
                            if a == 0 and q == 0:
                                wait_some(dve, y_done, nth(j, TILES, t - 1))
                            if a > 0:
                                dve.wait_ge(acc_seq, nth(j, 2 * TILES * len(BY_DVE), done - 1))
                            if a == 0 and q == 1:
                                ins = nc.vector.tensor_scalar(dst, src, scale, None, ALU.mult)
                            else:
                                ins = nc.vector.scalar_tensor_tensor(out=dst, in0=src, scalar=scale, in1=dst if a else x1[pj][:, t, :],
                                                                     op0=ALU.mult, op1=ALU.add)
                            ins.then_inc(acc_seq, 1)
                if kind == "E" and k % 2 == 1:
                    ex = k // 2
                    dve.wait_ge(e_high, ex + 1)
                    nc.vector.tensor_tensor(we_l[:, :, ex, :], stage[:, ex % STAGES, :].rearrange("p (c n) -> p c n", c=KC),
                                            we_h[:, :, ex, :].bitcast(F32), ALU.subtract).then_inc(e_split, 1)

            program(dve, step)

        @block.tensor
        def _(pe):
            pe.wait_ge(masks_up, 6)
            pe.wait_ge(zeroed, 3)

            def three(dst, pairs, close=True, opened=False):
                n = 0
                for w_high_, w_low_, x_high_, x_low_ in pairs:
                    for w, x in ((w_high_, x_high_), (w_high_, x_low_), (w_low_, x_high_)):
                        last = nc.tensor.matmul(dst, w, x, start=(n == 0 and not opened), stop=(close and n == 3 * len(pairs) - 1))
                        n += 1
                return last

            def step(tag, i, par, first, front, attend, experts):
                kind, k = tag
                mb = bank(tag, i, first, front) if kind in USES and (front if kind in IN_FRONT else attend) else None
                f = 0 if first else i + 1
                pf = 0 if first else 1 - par
                j, pj = i - 1, 1 - par
                if kind in USES and (front if kind in IN_FRONT else attend):
                    use = use_no(tag, i, first, front)
                    if kind == "T" and k == 0:
                        pe.wait_ge(xn_ready, nth(f, 1, 1))
                    if kind == "MT":
                        pe.wait_ge(max_done, nth(i, SUBS, k + 1))
                    if kind == "OT":
                        pe.wait_ge(o_done, nth(i, SUBS, 2 * k + 2))
                    if kind == "X2T":
                        pe.wait_ge(xn2_ready, nth(i, TILES, k + 1))
                    needs = {"KV": ("T", KC), "LT": ("X2T", TILES - 1), "LG": ("LT", 0), "WO": ("OT", k)}.get(kind)
                    c = i if isinstance(i, int) else 1
                    next_to = needs and use_no(tag, c, first, front) == use_no(needs, c, first, front) + 1
                    if next_to:
                        pe.wait_ge(misc_free, use)
                    elif not (isinstance(use, int) and use < 2):
                        pe.wait_ge(misc_free, use - 1)
                    if kind == "VT":
                        pe.wait_ge(k1_done, nth(f, 2, 2))
                    if tag in (("T", KC), ("VT", 0), ("LG", 0)):
                        pe.sem_inc(passed_pe, 1)
                if front and kind == "T":
                    if k < KC:
                        for n in range(TILES):
                            last = nc.tensor.transpose(mb[:, n * P:(n + 1) * P], xn[:, n, k * P:(k + 1) * P], ident[:, :])
                    else:
                        w = 2 * HALF
                        for c in range(KC):
                            last = nc.tensor.transpose(mb[:, c * w:(c + 1) * w], xn[0:w, TILES, c * P:(c + 1) * P], ident[0:w, 0:w])
                    last.then_inc(misc_full, 1)
                if front and kind == "Q":
                    three(mb[:, :], [(wq_h[:, c, k * P:(k + 1) * P], wq_l[:, c, k * P:(k + 1) * P],
                                        xT_h[:, c, HALF:HALF + BLOCK], xT_l[:, c, HALF:HALF + BLOCK]) for c in range(KC)]).then_inc(misc_full, 1)
                if front and kind == "KV":
                    if first:
                        pe.wait_ge(w_split, 4)
                        pe.wait_ge(b_high, 2)
                    h = HALO // 2
                    cols = slice(k * h, (k + 1) * h)
                    three(mb[:, 0:h], [(wkv_h[:, c, :], wkv_l[:, c, :], xT_h[:, c, cols], xT_l[:, c, cols]) for c in range(KC)], close=False)
                    nc.tensor.matmul(mb[:, 0:h], bkv_h[:, :], valid[:, pf * HALF + k * h:pf * HALF + (k + 1) * h], start=False, stop=False)
                    nc.tensor.matmul(mb[:, 0:h], bkv_l[:, :], valid[:, pf * HALF + k * h:pf * HALF + (k + 1) * h], start=False, stop=True).then_inc(misc_full, 1)
                if front and kind == "VT":
                    for c in range(SUBS):
                        last = nc.tensor.transpose(mb[:, c * 32:(c + 1) * 32], vT[32:64, c * SUB:c * SUB + P], ident[32:64, 32:64])
                    last.then_inc(misc_full, 1)
                if attend and kind == "S":
                    if k == 0:
                        pe.wait_ge(qk_in, nth(i, QK_LOADS, QK_LOADS))
                    if not (isinstance(i, int) and i == 0 and k == 0):
                        pe.wait_ge(max_done, nth(i, SUBS, k))
                    for a in range(PAIRS):
                        last = nc.tensor.matmul(s_ps[:, a, :], qst[par][0:ROWS, k, a * P:(a + 1) * P],
                                                kst[par][0:ROWS, a // (PAIRS // 2), k * SUB:k * SUB + P], start=True, stop=True)
                    last.then_inc(s_full, 1)
                if attend and kind == "MT":
                    nc.tensor.transpose(mb[0:PAIRS, 0:P], negmax[:, k % 2, :], ident[:, :]).then_inc(misc_full, 1)
                if attend and kind == "ST":
                    pe.wait_ge(m_in[k % 2], nth(i, 32 * SUBS // 2, 32 * (k // 2 + 1)))
                    if not (isinstance(i, int) and i == 0 and k == 0):
                        pe.wait_ge(exp_done, nth(i, SUBS, k))
                    for g in range(GROUPS):
                        nc.tensor.matmul(st_ps[:, g, :], kst[par][:, g, k * SUB:k * SUB + P],
                                         qst[par][:, k, g * 512:(g + 1) * 512], start=True, stop=False)
                        last = nc.tensor.matmul(st_ps[:, g, :], ident_b[:, :], far[:, :, :].rearrange("p h q -> p (h q)"), start=False, stop=True)
                    last.then_inc(st_full, 1)
                if attend and kind == "PV":
                    if k == 0:
                        pe.wait_ge(v3_done, nth(i, 1, 1))
                    pe.wait_ge(pl_done, nth(i, SUBS, k + 1))
                    for a in range(PAIRS):
                        v = v3[par][:, 2 * k + a // (PAIRS // 2), 0:VW]
                        nc.tensor.matmul(mb[:, a * VW:(a + 1) * VW], prob_h[:, a * P:(a + 1) * P], v, start=True, stop=False)
                        last = nc.tensor.matmul(mb[:, a * VW:(a + 1) * VW], prob_l[:, a * P:(a + 1) * P], v, start=False, stop=True)
                    last.then_inc(misc_full, 1)
                if attend and kind == "OT":
                    for s in range(2):
                        last = nc.tensor.transpose(mb[:, s * P:(s + 1) * P], o[:, (2 * k + s) % 4, :], ident[:, :])
                    last.then_inc(misc_full, 1)
                if attend and kind == "WO":
                    three(mb[:, 0:DIM], [(oT_h[:, r, :], oT_l[:, r, :], wo_h[:, r, :], wo_l[:, r, :]) for r in range(2)]).then_inc(misc_full, 1)
                if attend and kind == "X2T":
                    for c in range(KC):
                        last = nc.tensor.transpose(mb[:, c * P:(c + 1) * P], xn2[:, k % 2, c * P:(c + 1) * P], ident[:, :])
                    last.then_inc(misc_full, 1)
                if attend and kind == "LT":
                    n = 0
                    for c in range(KC):
                        for w in (wkv_h, wkv_l):
                            for x in (x2_h, x2_l):
                                last = nc.tensor.matmul(mb[:, :], w[:, c, :], x[par][:, c, :], start=(n == 0), stop=(n == 4 * KC - 1))
                                n += 1
                    last.then_inc(misc_full, 1)
                if attend and kind == "LG":
                    for t in range(TILES):
                        last = nc.tensor.transpose(mb[:, t * EXPERTS:(t + 1) * EXPERTS], lT[:, t * P:(t + 1) * P], ident[R0:R0 + EXPERTS, R0:R0 + EXPERTS])
                    last.then_inc(misc_full, 1)
                if kind == "M":
                    t, g = k // EG, k % EG
                    if k == 0 and isinstance(j, int) and j == 0:
                        pe.wait_ge(e_split, EXPERTS)
                    before = k - 2
                    if before >= 0 or not (isinstance(j, int) and j == 0):
                        tb, gb = before // EG, before % EG
                        if gb in BY_ACT:
                            pe.wait_ge(e_read_act, nth(j, TILES * len(BY_ACT), tb * len(BY_ACT) + BY_ACT.index(gb) + 1))
                        else:
                            pe.wait_ge(acc_seq, nth(j, 2 * TILES * len(BY_DVE), 2 * (tb * len(BY_DVE) + BY_DVE.index(gb) + 1)))
                    rows = slice(t * P, (t + 1) * P)
                    three(e_ps[:, k % 2, :], [(x2_h[pj][:, c, rows], x2_l[pj][:, c, rows], we_h[:, c, 2 * g:2 * g + 2, :], we_l[:, c, 2 * g:2 * g + 2, :])
                                              for c in range(KC)]).then_inc(e_full, 1)

            program(pe, step, LAGGING)




def kernel(L0_attn_x, L0_attn_Wq, L0_attn_bq, L0_attn_Wk, L0_attn_bk, L0_attn_Wv, L0_attn_bv, L0_attn_Wo, L0_attn_bo,
           L0_ffn_router_w, L0_ffn_router_b, L0_ffn_expert_w):
    import numpy as np
    import concourse.bacc as bacc
    from concourse.bass_utils import run_bass_kernel_spmd

    x = np.pad(np.asarray(L0_attn_x), ((0, 0), (HALF, HALF), (0, 0)))
    blocks = [x[b, s:s + HALO] for b in range(BATCH) for s in range(0, SEQ, BLOCK)]
    x_halo = np.stack(blocks + [np.zeros_like(blocks[0])])
    by_dim = (GROUPS, PER_GROUP, HD)
    wq = np.asarray(L0_attn_Wq).reshape(DIM, *by_dim).transpose(0, 1, 3, 2).reshape(DIM, DIM)
    bq = np.asarray(L0_attn_bq).reshape(by_dim).transpose(0, 2, 1).reshape(DIM)
    wo = np.asarray(L0_attn_Wo).reshape(PAIRS, 2, HD, DIM).transpose(1, 0, 2, 3).reshape(DIM, DIM)
    arrays = {
        "x_halo": x_halo, "wq": wq, "bq": bq, "wk": L0_attn_Wk, "bk": L0_attn_bk, "wv": L0_attn_Wv,
        "bv": L0_attn_bv, "wo": wo, "bo": L0_attn_bo, "rwt": np.asarray(L0_ffn_router_w).T,
        "rb": L0_ffn_router_b, "ew": L0_ffn_expert_w,
    }
    arrays = {k: np.ascontiguousarray(v) for k, v in arrays.items()}
    nc = bacc.Bacc("TRN2", target_bir_lowering=False, num_devices=1)
    args = [nc.dram_tensor(k, v.shape, mybir.dt.from_np(v.dtype), kind="ExternalInput").ap() for k, v in arrays.items()]
    out = nc.dram_tensor("out", (BLOCKS, BLOCK, DIM), F32, kind="ExternalOutput").ap()
    build(nc, *args, out)
    r = run_bass_kernel_spmd(nc, [arrays], core_ids=[0])
    return r.results[0]["out"].reshape(BATCH, SEQ, DIM)
```

```python
from contextlib import ExitStack

import concourse.bass as bass
from concourse import mybir

P = 128
DIM = 256
KC = DIM // P
HEADS = 16
GROUPS = 2
HD = DIM // HEADS
PER_GROUP = HEADS // GROUPS
WINDOW = 64
HALF = WINDOW // 2
BATCH, SEQ = 4, 1024
BLOCK = 512
HALO = BLOCK + 2 * HALF
BLOCKS = BATCH * SEQ // BLOCK
TILES = BLOCK // P
SUB = 64
SUBS = BLOCK // SUB
PAIRS = HEADS // 2
SLOTS_QK = 6
ROWS = SLOTS_QK * HD
MAXPARTS = 2
SLOTS_OF_PART = ((0, 1, 2), (3, 4), (5,))
VW = 3 * HD + 1
EXPERTS = 16
R0 = 2 * GROUPS * HD
R1 = R0 + 32
R2 = R1 + EXPERTS
TOP_K = 6
EPS_LN = 1e-5
EPS_GATE = 1e-10
FAR = -1e30
HUGE = 3e38
EG = EXPERTS // 2
BY_ACT = (1, 3, 5, 7)
BY_DVE = tuple(g for g in range(EG) if g not in BY_ACT)
STAGES = 4
QK_LOADS = 16 * (SLOTS_QK + len(SLOTS_OF_PART))

ALU = mybir.AluOpType
ACT = mybir.ActivationFunctionType
AX = mybir.AxisListType
F32 = mybir.dt.float32
F32R = mybir.dt.float32r
BF16 = mybir.dt.bfloat16
F16 = mybir.dt.float16
U8 = mybir.dt.uint8

FRONT_ORDER = [("LN1", 0), ("LN1", 1), ("LN1", 2), ("T", 0), ("T", 1), ("T", 2), ("E", 0), ("Q", 0), ("Q", 1),
               ("Qb", 0), ("Qb", 1), ("KV", 0), ("KV", 1), ("QL", 0), ("KVb", 0), ("VT", 0), ("VTb", 0), ("KL", 0)]
TAIL = [("OT", 3), ("WO", 3), ("XN", 3), ("X2T", 3), ("LT", 0), ("LG", 0)] + [("R", k) for k in range(7)]
SLOTS = [
    [("LN1", 0), ("LN1", 1)],
    [("S", 0), ("M",), ("OT", 3), ("MT", 0), ("LN1", 2), ("M",), ("M",), ("WO", 3)],
    [("S", 1), ("M",), ("T", 0), ("T", 1), ("ST", 0), ("M",), ("MT", 1)],
    [("S", 2), ("M",), ("XN", 3), ("T", 2), ("M",)],
    [("S", 3), ("MT", 2), ("X2T", 3), ("M",), ("ST", 1), ("M",), ("PV", 0), ("KV", 0), ("M",), ("KV", 1), ("LT", 0),
     ("KVb", 0), ("M",), ("MT", 3), ("ST", 2), ("LG", 0)],
    [("S", 4), ("R", 0), ("PV", 1), ("M",), ("VT", 0), ("R", 1), ("M",), ("MT", 4), ("R", 2), ("OT", 0), ("ST", 3), ("M",),
     ("R", 3), ("VTb", 0), ("R", 4), ("PV", 2), ("R", 5), ("Q", 0), ("M",)],
    [("S", 5), ("KL", 0), ("R", 6), ("Qb", 0), ("ST", 4), ("WO", 0), ("M",), ("Q", 1), ("M",), ("MT", 5)],
    [("S", 6), ("XN", 0), ("M",), ("M",), ("Qb", 1), ("MT", 6), ("PV", 3)],
    [("S", 7), ("M",), ("X2T", 0), ("OT", 1), ("ST", 5), ("M",), ("PV", 4), ("MT", 7), ("M",), ("WO", 1), ("ST", 6), ("M",),
     ("PV", 5), ("M",), ("XN", 1), ("QL", 0), ("X2T", 1), ("ST", 7), ("M",), ("OT", 2), ("M",), ("PV", 6), ("M",),
     ("WO", 2), ("M",), ("M",), ("XN", 2), ("PV", 7), ("X2T", 2), ("M",), ("M",), ("M",)],
]
FIRST_SLOTS = [
    [("LN1", 0), ("LN1", 1), ("E", 1), ("E", 2), ("E", 3), ("LN1", 2), ("E", 4), ("E", 5), ("E", 6), ("E", 7)],
    [("S", 0), ("T", 0), ("MT", 0)],
    [("S", 1), ("T", 1), ("T", 2), ("MT", 1), ("E", 8), ("E", 9)],
    [("S", 2), ("KV", 0), ("ST", 0), ("MT", 2), ("KV", 1), ("ST", 1)],
    [("S", 3), ("PV", 0)],
    [("S", 4), ("MT", 3), ("KVb", 0), ("E", 10), ("ST", 2), ("PV", 1), ("MT", 4), ("E", 11), ("E", 12), ("OT", 0),
     ("E", 13), ("VT", 0), ("VTb", 0), ("E", 14)],
    [("S", 5), ("Q", 0), ("WO", 0), ("ST", 3), ("E", 15), ("KL", 0), ("PV", 2), ("Qb", 0), ("Q", 1), ("XN", 0), ("MT", 5)],
    [("S", 6), ("ST", 4), ("E", 16), ("X2T", 0), ("PV", 3), ("E", 17), ("E", 18), ("MT", 6), ("E", 19)],
    [("S", 7), ("ST", 5), ("OT", 1), ("E", 20), ("Qb", 1), ("PV", 4), ("MT", 7), ("WO", 1), ("E", 21), ("ST", 6), ("E", 22),
     ("PV", 5), ("XN", 1), ("E", 23), ("X2T", 1), ("OT", 2), ("E", 24), ("E", 25), ("E", 26), ("ST", 7), ("WO", 2),
     ("E", 27), ("E", 28), ("E", 29), ("XN", 2), ("PV", 6), ("QL", 0), ("E", 30), ("E", 31), ("X2T", 2), ("PV", 7)],
]
ALL_GROUPS = TILES * EG
LAGGING = 15
ORDER, _m = [], 0
for _slot in SLOTS:
    for _tag in _slot:
        ORDER.append(_tag if _tag[0] != "M" else ("M", _m))
        _m += _tag[0] == "M"
assert _m == ALL_GROUPS, _m
FIRST_ORDER = [tag for slot in FIRST_SLOTS for tag in slot]
IN_FRONT = {t[0] for t in FRONT_ORDER}
USES = ("MT", "T", "Q", "KV", "VT", "PV", "OT", "WO", "X2T", "LT", "LG")
FRONT_USES = [t for t in FRONT_ORDER if t[0] in USES]
STEP_USES = [t for t in ORDER if t[0] in USES]
assert len(STEP_USES) % 2 == 0
FIRST_USES = [t for t in FIRST_ORDER if t[0] in USES]
TAIL_USES = [t for t in TAIL if t[0] in USES]
LAST_USES = [t for t in STEP_USES if t[0] not in IN_FRONT]


def nth(block, per, k):
    return block * per + k


P_STEPS = len(BY_ACT) + 1
R_STEPS = 16
R_ENDS = [2, 4, 6, 8, 10, 13]


def wait_some(e, sem, value):
    if not (isinstance(value, int) and value <= 0):
        e.wait_ge(sem, value)


def build(nc, x_halo, wq, bq, wk, bk, wv, bv, wo, bo, rwt, rb, ew, out):
    with ExitStack() as ctx:
        def sb(name, shape, dt):
            return ctx.enter_context(nc.sbuf_tensor(name, shape, dt))

        def ps(name, shape, dt=F32):
            return ctx.enter_context(nc.psum_tensor(name, shape, dt))

        def sem(name):
            return ctx.enter_context(nc.semaphore(name))

        q_dram = nc.dram_tensor("q_parts", [BLOCKS, 3, SUBS, GROUPS, P, SUB], BF16).ap()
        k_dram = nc.dram_tensor("k_parts", [BLOCKS, 3, GROUPS * HD, HALO], BF16).ap()

        s_ps = ps("s_ps", [P, PAIRS, P])
        st_ps = ps("st_ps", [P, GROUPS, 512])
        e_ps = ps("e_ps", [P, 2, 512])
        misc2 = ps("misc2", [P, 2, 512])

        stage = sb("stage", [P, STAGES, 512], F32)
        wq_h, wq_l = sb("wq_h", [P, KC, DIM], F32R), sb("wq_l", [P, KC, DIM], F32R)
        wkv_h, wkv_l = sb("wkv_h", [P, KC, P], F32R), sb("wkv_l", [P, KC, P], F32R)
        wo_h, wo_l = sb("wo_h", [P, 2, DIM], F32R), sb("wo_l", [P, 2, DIM], F32R)
        we_h = sb("we_h", [P, KC, EXPERTS, DIM], F32R)
        we_l = sb("we_l", [P, KC, EXPERTS, DIM], F32R)
        bq_c = sb("bq_c", [P, GROUPS], F32)
        bkv = sb("bkv", [1, 64], F32)
        bkv_h, bkv_l = sb("bkv_h", [1, P], F32R), sb("bkv_l", [1, P], F32R)
        bo_b = sb("bo_b", [P, DIM], F32)
        rb_c = sb("rb_c", [R2, 1], F32)
        valid = sb("valid", [1, HALO + HALF], F32R)
        ident = sb("ident", [P, P], F32)
        ident_b = sb("ident_b", [P, P], BF16)
        far = sb("far", [P, PER_GROUP, SUB], BF16)
        upper = sb("upper", [P, PAIRS, SUB], U8)
        expo = sb("expo", [P, 8], F32)
        eps = sb("eps", [P, 8], F32)
        xh = sb("xh", [P, TILES + 1, DIM], F32)
        st1 = sb("st1", [P, TILES + 1, 6], F32)
        mv1 = sb("mv1", [P, TILES + 1, 2], F32)
        ve1 = sb("ve1", [P, TILES + 1], F32)
        rstd1 = sb("rstd1", [P, TILES + 1], F32)
        xn = xh
        xT_h, xT_l = sb("xT_h", [P, KC, HALO], F32R), sb("xT_l", [P, KC, HALO], F32R)
        qp = sb("qp", [P, 3, SUBS, GROUPS, SUB], BF16)
        rq = sb("rq", [P, GROUPS, BLOCK], F32)
        kp = sb("kp", [GROUPS * HD, 3, HALO], BF16)
        rq_flat = rq[:, :, :].rearrange("p g t -> p (g t)")
        rk = rq_flat[0:GROUPS * HD, 0:HALO]
        rv = rq_flat[:, HALO:HALO + SUBS * GROUPS * HD].rearrange("p (c d) -> p c d", d=HD)
        rows64 = sb("rows64", [R2, HALO], F32)
        vT = rows64
        lT = rows64[R0:R2, 0:BLOCK]
        qst = [sb(f"qst{p}", [ROWS + MAXPARTS, SUBS, GROUPS * 512], BF16) for p in range(2)]
        kst = [sb(f"kst{p}", [ROWS + MAXPARTS, GROUPS, HALO], BF16) for p in range(2)]
        v3 = [sb(f"v3{p}", [P, SUBS * GROUPS, VW + 1], BF16) for p in range(2)]
        negmax = sb("negmax", [P, 2, PAIRS], F32)
        mp = sb("mp", [PAIRS, 2, MAXPARTS, P], BF16)
        prob = sb("prob", [P, GROUPS * 512], F32)
        prob_h, prob_l = sb("prob_h", [P, GROUPS * 512], F16), sb("prob_l", [P, GROUPS * 512], F16)
        upper_f = prob[:, 0:PAIRS * SUB // 2].bitcast(BF16).rearrange("p (a q) -> p a q", a=PAIRS)
        osum = sb("osum", [P, PAIRS, HD], F32)
        rden = sb("rden", [P, PAIRS], F32)
        o = sb("o", [P, 4, PAIRS * HD], F32)
        oT_h, oT_l = sb("oT_h", [P, 2, P], F32R), sb("oT_l", [P, 2, P], F32R)
        x1 = [sb(f"x1{p}", [P, TILES, DIM], F32) for p in range(2)]
        st2 = sb("st2", [P, 2, 6], F32)
        mv2 = sb("mv2", [P, 2, 2], F32)
        ve2 = sb("ve2", [P, 2], F32)
        rstd2 = sb("rstd2", [P, 2], F32)
        xn2 = sb("xn2", [P, 2, DIM], F32)
        x2_h = [sb(f"x2_h{p}", [P, KC, BLOCK], F32R) for p in range(2)]
        x2_l = [sb(f"x2_l{p}", [P, KC, BLOCK], F32R) for p in range(2)]
        lg = sb("lg", [P, TILES, EXPERTS + 8], F32)
        m8 = sb("m8", [P, TILES, 8], F32)
        ld = sb("ld", [P, TILES, EXPERTS], F32)
        le = sb("le", [P, TILES, EXPERTS], F32)
        rep = sb("rep", [P, TILES, EXPERTS + 8], F32)
        sel = sb("sel", [P, TILES, EXPERTS], F32)
        z = sb("z", [P, 6, TILES], F32)
        gate = [sb(f"gate{p}", [P, TILES, EXPERTS], F32) for p in range(2)]
        etop = [sb(f"etop{p}", [P, TILES], F32) for p in range(2)]
        acc = sb("acc", [P, 2, 2, DIM], F32)
        tmp = stage[:, 0:2, :]
        acc_p = stage[:, 2, :]
        y = stage[:, 3, :].rearrange("p (a n) -> p a n", a=2)

        w_in = sem("w_in")
        b_in = sem("b_in")
        e_in = [sem(f"e_in{k}") for k in range(STAGES)]
        w_high = sem("w_high")
        w_split = sem("w_split")
        e_high = sem("e_high")
        e_split = sem("e_split")
        b_high = sem("b_high")
        zeroed = sem("zeroed")
        ones_up = sem("ones_up")
        masks_up = sem("masks_up")
        masks_ok = sem("masks_ok")
        x_in = sem("x_in")
        xres_in = sem("xres_in")
        ln1_stat, ln1_mv = sem("ln1_stat"), sem("ln1_mv")
        ln1_ve, ln1_rstd = sem("ln1_ve"), sem("ln1_rstd")
        xn_ready = sem("xn_ready")
        misc_full = sem("misc_full")
        misc_free = sem("misc_free")
        xT_high = sem("xT_high")
        q1_done, q2_done = sem("q1_done"), sem("q2_done")
        q3_done = sem("q3_done")
        q_out = [sem(f"q_out{s}") for s in range(3)]
        k1_done = sem("k1_done")
        k2_done = sem("k2_done")
        k3_done = sem("k3_done")
        k_out = sem("k_out")
        v1_done, v2_done = sem("v1_done"), sem("v2_done")
        v3_done = sem("v3_done")
        qk_in = sem("qk_in")
        s_full = sem("s_full")
        s_sel = sem("s_sel")
        max_done = sem("max_done")
        m1_done = sem("m1_done")
        m_in = [sem(f"m_in{p}") for p in range(2)]
        st_full = sem("st_full")
        exp_done = sem("exp_done")
        ph_done = sem("ph_done")
        pl_done = sem("pl_done")
        o_done = sem("o_done")
        oT_high = sem("oT_high")
        xb_ready = sem("xb_ready")
        ln2_stat, ln2_mv = sem("ln2_stat"), sem("ln2_mv")
        ln2_ve, ln2_rstd = sem("ln2_ve"), sem("ln2_rstd")
        xn2_ready = sem("xn2_ready")
        x2_high = sem("x2_high")
        r_seq = sem("r_seq")
        r_exp = sem("r_exp")
        gates_ready = sem("gates_ready")
        e_full = sem("e_full")
        e_read_act = sem("e_read_act")
        acc_seq = sem("acc_seq")
        p_seq = sem("p_seq")
        y_done = sem("y_done")
        passed_dve, passed_pe = sem("passed_dve"), sem("passed_pe")
        y_out = [sem(f"y_out{p}") for p in range(2)]

        def use_no(tag, i, first, front):
            if first:
                return FRONT_USES.index(tag)
            if tag in TAIL:
                i = i + 1
            if isinstance(i, int) and i == 0:
                return len(FRONT_USES) + FIRST_USES.index(tag)
            if isinstance(i, int) and i == BLOCKS:
                done = TAIL_USES.index(tag)
                return nth(i - 1, len(STEP_USES), len(FRONT_USES) - len(TAIL_USES)) + len(LAST_USES) + done
            uses = LAST_USES if isinstance(i, int) and i == BLOCKS - 1 else STEP_USES
            return nth(i, len(STEP_USES), len(FRONT_USES) - len(TAIL_USES) + uses.index(tag))

        def pv_before(i, k):
            return (use_no(("PV", k - 1), i, False, True) if k else use_no(("PV", SUBS - 1), i - 1, False, True)) + 1

        def bank(tag, i, first, front):
            if not isinstance(i, int):
                i = 1
            return misc2[:, use_no(tag, i, first, front) % 2, :]

        def by_sub(t):
            return t.rearrange("p (u q) -> p u q", q=SUB)

        block = ctx.enter_context(nc.Block())

        def tile_before(k, j, pj, g):
            if k % EG != g or (isinstance(j, int) and j == 0 and k < EG):
                return None
            return (j, pj, k // EG - 1) if k >= EG else (j - 1, 1 - pj, TILES - 1)

        def program(e, step, lagging=LAGGING + 1):
            def one(i, par, front=True, attend=True, behind=2):
                for tag in ORDER if behind else FIRST_ORDER:
                    if tag[0] == "M":
                        lag = 2 if tag[1] < lagging else 1
                        if lag <= behind:
                            step(("M", (tag[1] - lagging) % ALL_GROUPS), i - lag + 1, (par + lag + 1) % 2,
                                 first=False, front=False, attend=False)
                    elif tag in TAIL:
                        if behind:
                            step(tag, i - 1, 1 - par, first=False, front=False, attend=True)
                    elif attend:
                        step(tag, i, par, first=False, front=front, attend=True)

            for tag in FRONT_ORDER:
                step(tag, 0, 1, first=True, front=True, attend=False)
            one(0, 0, behind=0)
            one(1, 1, behind=1)
            with e.Fori(1, BLOCKS // 2 - 1) as n:
                for half in range(2):
                    one(n * 2 + half, half)
            one(BLOCKS - 2, 0)
            one(BLOCKS - 1, 1, front=False)
            one(BLOCKS, 0, front=False, attend=False)
            for k in range(ALL_GROUPS - lagging, ALL_GROUPS):
                step(("M", k), BLOCKS, 0, first=False, front=False, attend=False)
            step(("END", 0), BLOCKS, 0, first=False, front=False, attend=False)

        @block.sync
        def _(sp):
            sp.dma_start(xh[:, 0:TILES, :], x_halo[0, 0:BLOCK, :].rearrange("(t p) d -> p t d", p=P)).then_inc(x_in, 16)
            sp.dma_start(xh[0:2 * HALF, TILES, :], x_halo[0, BLOCK:HALO, :]).then_inc(x_in, 16)
            sp.dma_start(stage[:, 0, :].rearrange("p (c n) -> p c n", c=KC),
                         wq.rearrange("(c p) n -> p c n", p=P)).then_inc(w_in, 16)
            kv = stage[:, 1, 0:KC * 64].rearrange("p (c n) -> p c n", c=KC)
            sp.dma_start(kv[:, :, 0:32], wk.rearrange("(c p) n -> p c n", p=P)).then_inc(w_in, 16)
            sp.dma_start(kv[:, :, 32:64], wv.rearrange("(c p) n -> p c n", p=P)).then_inc(w_in, 16)
            sp.dma_start(stage[:, 2, :].rearrange("p (c n) -> p c n", c=2), wo.rearrange("(c p) n -> p c n", p=P)).then_inc(w_in, 16)
            sp.dma_start(stage[:, 3, 0:KC * EXPERTS].rearrange("p (c n) -> p c n", c=KC),
                         rwt.rearrange("(c p) n -> p c n", p=P)).then_inc(w_in, 16)
            for g in range(GROUPS):
                sp.dma_start(bq_c[:, g:g + 1], bq.rearrange("(n a) -> n a", a=1)[g * P:(g + 1) * P, :]).then_inc(b_in, 16)
            sp.dma_start(bkv[:, 0:32], bk.rearrange("(a n) -> a n", a=1)).then_inc(b_in, 16)
            sp.dma_start(bkv[:, 32:64], bv.rearrange("(a n) -> a n", a=1)).then_inc(b_in, 16)
            sp.dma_start(bo_b[:, :], bo.rearrange("(a n) -> a n", a=1).broadcast_to([P, DIM])).then_inc(b_in, 16)
            sp.wait_ge(zeroed, 1)
            sp.dma_start(rb_c[R0:R0 + EXPERTS, :], rb.rearrange("(n a) -> n a", a=1)).then_inc(b_in, 16)

            def step(tag, i, par, first, front, attend):
                kind, k = tag
                f = 0 if first else i + 1
                pf = 0 if first else 1 - par
                if front and tag == ("T", 2):
                    g = f + 1
                    sp.wait_ge(misc_free, use_no(tag, i, first, front) + 1)
                    sp.dma_start(xh[:, 0:TILES, :], x_halo[g, 0:BLOCK, :].rearrange("(t p) d -> p t d", p=P)).then_inc(x_in, 16)
                    sp.dma_start(xh[0:2 * HALF, TILES, :], x_halo[g, BLOCK:HALO, :]).then_inc(x_in, 16)
                if attend and kind == "S" and k == 3:
                    if not (isinstance(i, int) and i < 2):
                        sp.wait_ge(acc_seq, nth(i - 2, 2 * TILES * len(BY_DVE), 2 * (TILES - 1) * len(BY_DVE) + 1))
                    sp.dma_start(x1[par][:, :, :], x_halo[i, HALF:HALF + BLOCK, :].rearrange("(t p) d -> p t d", p=P)).then_inc(xres_in, 16)
                if attend and kind == "MT":
                    sp.wait_ge(misc_free, use_no(tag, i, first, front) + 1)
                    for part in range(MAXPARTS):
                        sp.dma_start(qst[par][ROWS + part:ROWS + part + 1, k, :], mp[:, k % 2, part, :]).then_inc(m_in[k % 2], 16)
                if front and tag == ("Qb", 1):
                    for part, done in enumerate((q1_done, q2_done, q3_done)):
                        sp.wait_ge(done, nth(f, 2, 2))
                        sp.dma_start(q_dram[f, part].rearrange("u g p q -> p (u g) q"),
                                     qp[:, part, :, :, :].rearrange("p u g q -> p (u g) q")).then_inc(q_out[part], 16)
                if front and kind == "QL":
                    for part, slots in enumerate(SLOTS_OF_PART):
                        sp.wait_ge(q_out[part], nth(f, 16, 16))
                        for s in slots:
                            sp.dma_start(qst[pf][s * HD:(s + 1) * HD, :, :].rearrange("d u (g c) -> d (u g) c", g=GROUPS),
                                         q_dram[f, part].rearrange("u g (d h) q -> d (u g) (h q)", d=HD)).then_inc(qk_in, 16)
                if front and kind == "KVb":
                    sp.wait_ge(k3_done, nth(f, 1, 1))
                    sp.dma_start(k_dram[f].rearrange("s p t -> p s t"), kp[:, :, :]).then_inc(k_out, 16)
                if front and kind == "KL":
                    sp.wait_ge(k_out, nth(f, 16, 16))
                    for slots in SLOTS_OF_PART:
                        n = len(slots)
                        sp.dma_start(kst[pf][slots[0] * HD:(slots[0] + n) * HD, :, :].rearrange("p g t -> p (g t)"),
                                     k_dram[f, 0:n].rearrange("s (d g) t -> (s d) (g t)", g=GROUPS)).then_inc(qk_in, 16)
                if kind == "E" and k % 2 == 0:
                    if k == 0:
                        sp.wait_ge(w_split, 4)
                    for ex in range(STAGES) if k == 0 else range(k // 2 + STAGES - 1, min(k // 2 + STAGES, EXPERTS)):
                        if k > 0:
                            sp.wait_ge(e_split, ex - STAGES + 1)
                        sp.dma_start(stage[:, ex % STAGES, :].rearrange("p (c n) -> p c n", c=KC),
                                     ew[ex].rearrange("(c p) n -> p c n", p=P)).then_inc(e_in[ex % STAGES], 16)

                late = (BLOCKS - 1, 1, TILES - 1) if kind == "END" else tile_before(k, i - 1, 1 - par, 4) if kind == "M" else None
                if late:
                    j, _, t = late
                    sp.wait_ge(y_done, nth(j, TILES, t + 1))
                    sp.dma_start(out[j, t * P:(t + 1) * P, :], y[:, t % 2, :]).then_inc(y_out[t % 2], 16)

            program(sp, step)
            for p in range(2):
                sp.wait_ge(y_out[p], 16 * BLOCKS * TILES // 2)

        @block.gpsimd
        def _(pool):
            nc.gpsimd.memset(ident[:, :], 0.0).then_inc(ones_up, 1)
            nc.gpsimd.memset(ident_b[:, :], 0.0).then_inc(ones_up, 1)
            nc.gpsimd.memset(far[:, :, :], 0.0).then_inc(ones_up, 1)
            nc.gpsimd.memset(upper_f[:, :, :], 1.0).then_inc(ones_up, 1)
            nc.gpsimd.memset(expo[:, :], -0.5).then_inc(ones_up, 1)
            nc.gpsimd.memset(eps[:, :], EPS_LN).then_inc(ones_up, 1)
            pool.wait_ge(ones_up, 6)
            for t in (ident, ident_b):
                nc.gpsimd.affine_select(out=t[:, :], in_=t[:, :], compare_op=ALU.not_equal, fill=1.0, base=0,
                                        pattern=[[-1, P]], channel_multiplier=1).then_inc(masks_up, 1)
            nc.gpsimd.affine_select(out=far[:, :, :], in_=far[:, :, :], compare_op=ALU.is_ge, fill=FAR, base=0,
                                    pattern=[[0, PER_GROUP], [-1, SUB]], channel_multiplier=1).then_inc(masks_up, 1)
            pool.wait_ge(masks_up, 3)
            nc.gpsimd.affine_select(out=far[:, :, :], in_=far[:, :, :], compare_op=ALU.is_ge, fill=FAR, base=WINDOW - 1,
                                    pattern=[[0, PER_GROUP], [1, SUB]], channel_multiplier=-1).then_inc(masks_up, 1)
            for r in range(2):
                pool.wait_ge(masks_up, 4 + r)
                part = upper_f[r * SUB:(r + 1) * SUB, :, :]
                nc.gpsimd.affine_select(out=part, in_=part, compare_op=ALU.is_gt, fill=0.0, base=0,
                                        pattern=[[0, PAIRS], [-1, SUB]], channel_multiplier=1).then_inc(masks_up, 1)
            pool.wait_ge(masks_up, 6)

            def step(tag, i, par, first, front, attend):
                kind, k = tag
                f = 0 if first else i + 1
                pf = 0 if first else 1 - par
                j, pj = i - 1, 1 - par
                if front and tag == ("LN1", 1):
                    pool.wait_ge(ln1_mv, nth(f, 1, 1))
                    nc.gpsimd.tensor_tensor(ve1[:, :], mv1[:, :, 1], eps[:, 0:TILES + 1], ALU.add).then_inc(ln1_ve, 1)
                    pool.wait_ge(ln1_ve, nth(f, 1, 1))
                    nc.gpsimd.tensor_tensor(rstd1[:, :], ve1[:, :], expo[:, 0:TILES + 1], ALU.pow).then_inc(ln1_rstd, 1)
                if attend and tag == ("PV", 1):
                    pool.wait_ge(xres_in, nth(i, 16, 16))
                    if isinstance(i, int) and i == 0:
                        pool.wait_ge(b_in, 16 * 6)
                    nc.gpsimd.tensor_tensor(x1[par][:, :, :], x1[par][:, :, :], bo_b[:, :].rearrange("p (a n) -> p a n", a=1).broadcast_to([P, TILES, DIM]),
                                            ALU.add).then_inc(xb_ready, 1)
                if attend and (tag == ("ST", 0) or kind == "PV" and k < SUBS - 1):
                    k = 0 if kind == "ST" else k + 1
                    pool.wait_ge(ph_done, nth(i, SUBS, k + 1))
                    nc.gpsimd.tensor_tensor(prob_l[:, :], prob[:, :], prob_h[:, :], ALU.subtract).then_inc(pl_done, 1)
                if attend and kind == "WO":
                    pool.wait_ge(ln2_mv, nth(i, TILES, k + 1))
                    nc.gpsimd.tensor_tensor(ve2[:, k % 2:k % 2 + 1], mv2[:, k % 2, 1:2], eps[:, 0:1], ALU.add).then_inc(ln2_ve, 1)
                    pool.wait_ge(ln2_ve, nth(i, TILES, k + 1))
                    nc.gpsimd.tensor_tensor(rstd2[:, k % 2:k % 2 + 1], ve2[:, k % 2:k % 2 + 1], expo[:, 0:1], ALU.pow).then_inc(ln2_rstd, 1)
                if front and kind == "Qb":
                    pool.wait_ge(q2_done, nth(f, 2, k + 1))
                    if not first:
                        pool.wait_ge(q_out[2], nth(f, 16, 0))
                    nc.gpsimd.tensor_tensor(qp[:, 2, :, k, :], by_sub(rq[:, k, :]), qp[:, 1, :, k, :], ALU.subtract).then_inc(q3_done, 1)
                if front and kind == "KVb":
                    pool.wait_ge(k2_done, nth(f, 1, 1))
                    nc.gpsimd.tensor_tensor(kp[:, 2, :], rk[:, :], kp[:, 1, :], ALU.subtract).then_inc(k3_done, 1)
                if front and kind == "VTb":
                    pool.wait_ge(v2_done, nth(f, 1, 1))
                    nc.gpsimd.tensor_tensor(v3[pf][:, :, 2 * HD:3 * HD], rv[:, :, :], v3[pf][:, :, HD:2 * HD],
                                            ALU.subtract).then_inc(v3_done, 1)
                late = (BLOCKS - 1, 1, TILES - 1) if kind == "END" else tile_before(k, j, pj, 1) if kind == "M" else None
                if late:
                    lj, _, t = late
                    pool.wait_ge(p_seq, nth(lj, P_STEPS * TILES, P_STEPS * t + len(BY_ACT) - 1))
                    wait_some(pool, y_out[t % 2], nth(lj, 16 * TILES // 2, 16 * (t // 2)))
                    nc.gpsimd.tensor_tensor(y[:, t % 2, :], acc_p[:, 0:DIM], acc_p[:, DIM:2 * DIM], ALU.add).then_inc(p_seq, 1)
                    pool.wait_ge(acc_seq, nth(lj, 2 * TILES * len(BY_DVE), 2 * (t + 1) * len(BY_DVE)))
                    for q in range(2):
                        pool.wait_ge(p_seq, nth(lj, P_STEPS * TILES, P_STEPS * t + len(BY_ACT) + q))
                        nc.gpsimd.tensor_tensor(y[:, t % 2, :], y[:, t % 2, :], acc[:, t % 2, q, :], ALU.add).then_inc((p_seq, y_done)[q], 1)
                if kind == "M" and k % EG in BY_ACT[1:]:
                    t, a = k // EG, BY_ACT.index(k % EG)
                    pool.wait_ge(e_read_act, nth(j, TILES * len(BY_ACT), t * len(BY_ACT) + a + 1))
                    wait_some(pool, p_seq, nth(j, P_STEPS * TILES, P_STEPS * t + (a - 1 if a > 1 else len(BY_ACT) - P_STEPS)))
                    nc.gpsimd.tensor_tensor(acc_p[:, :], tmp[:, 0, :] if a == 1 else acc_p[:, :], tmp[:, a % 2, :], ALU.add).then_inc(p_seq, 1)

            program(pool, step)

        @block.scalar
        def _(act):
            act.wait_ge(w_in, 16 * 5)
            act.wait_ge(zeroed, 1)
            for dst, src in ((wq_h[:, :, :], stage[:, 0, :].rearrange("p (c n) -> p c n", c=KC)),
                             (wkv_h[:, :, 0:64], stage[:, 1, 0:KC * 64].rearrange("p (c n) -> p c n", c=KC)),
                             (wo_h[:, :, :], stage[:, 2, :].rearrange("p (c n) -> p c n", c=2)),
                             (wkv_h[:, :, R0:R0 + EXPERTS], stage[:, 3, 0:KC * EXPERTS].rearrange("p (c n) -> p c n", c=KC))):
                nc.scalar.activation(dst, src, ACT.Copy).then_inc(w_high, 1)
            act.wait_ge(b_in, 16 * 6)
            nc.scalar.activation(bkv_h[:, 0:64], bkv[:, :], ACT.Copy).then_inc(b_high, 1)

            def step(tag, i, par, first, front, attend):
                kind, k = tag
                mb = bank(tag, i, first, front) if kind in USES and (front if kind in IN_FRONT else attend) else None
                f = 0 if first else i + 1
                pf = 0 if first else 1 - par
                j, pj = i - 1, 1 - par
                if kind in USES and (front if kind in IN_FRONT else attend):
                    act_waits_misc = kind not in ("MT", "PV", "WO", "LT", "LG")
                    if act_waits_misc:
                        act.wait_ge(misc_full, use_no(tag, i, first, front) + 1)
                if front and kind == "T":
                    if k < KC:
                        nc.scalar.activation(xT_h[:, k, 0:BLOCK], mb[:, :], ACT.Copy).then_inc(xT_high, 1)
                    else:
                        nc.scalar.activation(xT_h[:, :, BLOCK:HALO],
                                             mb[:, 0:KC * 2 * HALF].rearrange("p (c n) -> p c n", c=KC), ACT.Copy).then_inc(xT_high, 1)
                if front and kind == "Q":
                    if not first:
                        act.wait_ge(q_out[0], nth(f, 16, 0))
                    nc.scalar.activation(qp[:, 0, :, k, :], by_sub(mb[:, :]), ACT.Identity, bias=bq_c[:, k:k + 1]).then_inc(q1_done, 1)
                    act.wait_ge(misc_free, use_no(tag, i, first, front) + 1)
                    if not first:
                        act.wait_ge(q_out[1], nth(f, 16, 0))
                    nc.scalar.activation(qp[:, 1, :, k, :], by_sub(rq[:, k, :]), ACT.Copy).then_inc(q2_done, 1)
                if front and kind == "KV":
                    h = HALO // 2
                    if not first:
                        act.wait_ge(k_out, nth(f, 16, 0))
                    nc.scalar.activation(kp[:, 0, k * h:(k + 1) * h], mb[0:32, 0:h], ACT.Copy)
                    nc.scalar.activation(vT[32:64, k * h:(k + 1) * h], mb[32:64, 0:h], ACT.Copy).then_inc(k1_done, 1)
                    if k == 1:
                        act.wait_ge(misc_free, use_no(tag, i, first, front) + 1)
                        nc.scalar.activation(kp[:, 1, :], rk[:, :], ACT.Copy).then_inc(k2_done, 1)
                if front and kind == "VT":
                    nc.scalar.activation(v3[pf][:, :, 0:HD], mb[:, 0:SUBS * 32].rearrange("p (c d) -> p c d", d=HD),
                                         ACT.Copy).then_inc(v1_done, 1)
                    act.wait_ge(misc_free, use_no(tag, i, first, front) + 1)
                    nc.scalar.activation(v3[pf][:, :, HD:2 * HD], rv[:, :, :], ACT.Copy).then_inc(v2_done, 1)
                if attend and kind == "ST":
                    act.wait_ge(st_full, nth(i, SUBS, k + 1))
                    if not (isinstance(i, int) and i == 0 and k == 0):
                        act.wait_ge(pl_done, nth(i, SUBS, k))
                    nc.scalar.activation(prob[:, :], st_ps[:, :, :].rearrange("p g n -> p (g n)"), ACT.Exp).then_inc(exp_done, 1)
                if attend and (tag == ("ST", 0) or kind == "PV" and k < SUBS - 1):
                    n = 0 if kind == "ST" else k + 1
                    act.wait_ge(exp_done, nth(i, SUBS, n + 1))
                    if not (isinstance(i, int) and i == 0 and n == 0):
                        act.wait_ge(misc_full, pv_before(i, n))
                    nc.scalar.activation(prob_h[:, :], prob[:, :], ACT.Copy).then_inc(ph_done, 1)
                if attend and kind == "OT":
                    nc.scalar.activation(oT_h[:, :, :].rearrange("p r (s q) -> p s r q", s=2),
                                         mb[:, 0:2 * P].rearrange("p (s r q) -> p s r q", s=2, r=2), ACT.Copy).then_inc(oT_high, 1)
                if attend and kind == "X2T":
                    nc.scalar.activation(x2_h[par][:, :, k * P:(k + 1) * P], mb[:, 0:KC * P].rearrange("p (c n) -> p c n", c=KC),
                                         ACT.Copy).then_inc(x2_high, 1)
                if attend and tag == ("R", 1):
                    act.wait_ge(r_seq, nth(i, R_STEPS, 2))
                    nc.scalar.activation(le[:, :, :], ld[:, :, :], ACT.Exp).then_inc(r_exp, 1)
                if kind == "M":
                    t, g = k // EG, k % EG
                    if g in BY_ACT:
                        a = BY_ACT.index(g)
                        act.wait_ge(e_full, nth(j, TILES * EG, k + 1))
                        act.wait_ge(gates_ready, nth(j, 1, 1))
                        before = max(1, a - 2) if a >= 2 else len(BY_ACT) - 1 - (len(BY_ACT) - 1 - a) % 2 - P_STEPS
                        wait_some(act, p_seq, nth(j, P_STEPS * TILES, P_STEPS * t + before))
                        for q in range(2):
                            scale = gate[pj][:, t, 2 * g + q:2 * g + q + 1]
                            src, dst = e_ps[:, k % 2, q * DIM:(q + 1) * DIM], tmp[:, a % 2, q * DIM:(q + 1) * DIM]
                            if a == 0 and q == 0:
                                last = nc.scalar.activation(dst, src, ACT.Identity, scale=scale, bias=etop[pj][:, t:t + 1])
                            else:
                                last = nc.scalar.activation(dst, src, ACT.Copy, scale=scale)
                        last.then_inc(e_read_act, 1)
                if kind == "E" and k % 2 == 1:
                    ex = k // 2
                    act.wait_ge(e_in[ex % STAGES], 16 * (ex // STAGES + 1))
                    nc.scalar.activation(we_h[:, :, ex, :], stage[:, ex % STAGES, :].rearrange("p (c n) -> p c n", c=KC),
                                         ACT.Copy).then_inc(e_high, 1)

            program(act, step)

        @block.vector
        def _(dve):
            nc.vector.memset(xh[2 * HALF:P, TILES, :], 0.0)
            nc.vector.memset(rb_c[R0:R2, :], 0.0)
            nc.vector.memset(lg[:, :, EXPERTS:], -HUGE)
            for t in (wkv_h, wkv_l):
                nc.vector.memset(t[:, :, :].bitcast(F32), 0.0)
            nc.vector.memset(bkv_h[:, :].bitcast(F32), 0.0)
            nc.vector.memset(bkv_l[:, :].bitcast(F32), 0.0).then_inc(zeroed, 1)
            nc.vector.memset(valid[:, :].bitcast(F32), 1.0).then_inc(zeroed, 1)
            dve.wait_ge(zeroed, 2)
            nc.vector.memset(valid[:, 0:HALF].bitcast(F32), 0.0)
            nc.vector.memset(valid[:, HALO:HALO + HALF].bitcast(F32), 0.0).then_inc(zeroed, 1)
            def split_weights():
                for n, (dst, src, high) in enumerate((
                        (wq_l[:, :, :], stage[:, 0, :].rearrange("p (c n) -> p c n", c=KC), wq_h[:, :, :]),
                        (wkv_l[:, :, 0:64], stage[:, 1, 0:KC * 64].rearrange("p (c n) -> p c n", c=KC), wkv_h[:, :, 0:64]),
                        (wo_l[:, :, :], stage[:, 2, :].rearrange("p (c n) -> p c n", c=2), wo_h[:, :, :]),
                        (wkv_h[:, :, R1:R2], stage[:, 3, 0:KC * EXPERTS].rearrange("p (c n) -> p c n", c=KC), wkv_h[:, :, R0:R0 + EXPERTS]))):
                    dve.wait_ge(w_high, n + 1)
                    nc.vector.tensor_tensor(dst, src, high.bitcast(F32), ALU.subtract).then_inc(w_split, 1)
                dve.wait_ge(b_high, 1)
                nc.vector.tensor_tensor(bkv_l[:, 0:64], bkv[:, :], bkv_h[:, 0:64].bitcast(F32), ALU.subtract).then_inc(b_high, 1)
                dve.wait_ge(masks_up, 6)
                nc.vector.tensor_copy(upper[:, :, :], upper_f[:, :, :]).then_inc(masks_ok, 1)
                dve.wait_ge(masks_ok, 1)

            def settled():
                dve.sem_inc(passed_dve, 1)

            def ln1(f, part):
                if part == 0:
                    dve.wait_ge(x_in, nth(f, 32, 32))
                for n in ((0, 1, 2), (3, 4), ())[part]:
                    last = nc.vector.bn_stats(st1[:, n, :], xh[:, n, :])
                if part == 1:
                    last.then_inc(ln1_stat, 1)
                    dve.wait_ge(ln1_stat, nth(f, 1, 1))
                    settled()
                    for n in range(TILES + 1):
                        last = nc.vector.bn_aggr(mv1[:, n, :], st1[:, n, :])
                    last.then_inc(ln1_mv, 1)
                if part == 2:
                    dve.wait_ge(ln1_rstd, nth(f, 1, 1))
                    for n in range(TILES + 1):
                        last = nc.vector.tensor_scalar(xn[:, n, :], xh[:, n, :], mv1[:, n, 0:1], rstd1[:, n:n + 1],
                                                       ALU.subtract, ALU.mult)
                    last.then_inc(xn_ready, 1)

            def router(i, par, part):
                def link(n, ins):
                    ins.then_inc(r_seq, 1)
                    if n < R_STEPS and n not in R_ENDS:
                        dve.wait_ge(r_seq, nth(i, R_STEPS, n))

                def wide(v):
                    return v.broadcast_to([P, TILES, EXPERTS])

                def z_(n):
                    return z[:, n, :].rearrange("p (t a) -> p t a", a=1)

                if part == 0:
                    dve.wait_ge(misc_free, use_no(("LG", 0), i, False, False) + 1)
                    settled()
                    for t in range(TILES):
                        last = nc.vector.max(m8[:, t, :], lg[:, t, 0:EXPERTS])
                    link(1, last)
                    link(2, nc.vector.tensor_tensor(ld[:, :, :], lg[:, :, 0:EXPERTS], wide(m8[:, :, 0:1]), ALU.subtract))
                else:
                    dve.wait_ge(r_seq, nth(i, R_STEPS, R_ENDS[part - 1]))
                if part == 1:
                    link(3, nc.vector.memset(m8[:, :, TOP_K:8], -HUGE))
                    settled()
                    for t in range(TILES):
                        last = nc.vector.match_replace(rep[:, t, :], m8[:, t, :], lg[:, t, :], HUGE)
                    link(4, last)
                if part == 2:
                    link(5, nc.vector.tensor_scalar(sel[:, :, :], rep[:, :, 0:EXPERTS], HUGE, None, ALU.is_equal))
                    dve.wait_ge(r_exp, nth(i, 1, 1))
                    link(6, nc.vector.tensor_reduce(z[:, 1, :], le[:, :, :], AX.X, ALU.add))
                if part == 3:
                    link(7, nc.vector.reciprocal(z[:, 2, :], z[:, 1, :]))
                    link(8, nc.vector.tensor_tensor(ld[:, :, :], le[:, :, :], wide(z_(2)), ALU.mult))
                if part == 4:
                    link(9, nc.vector.tensor_tensor(sel[:, :, :], sel[:, :, :], ld[:, :, :], ALU.mult))
                    link(10, nc.vector.tensor_reduce(z[:, 3, :], sel[:, :, :], AX.X, ALU.add))
                if part == 5:
                    link(11, nc.vector.tensor_scalar(z[:, 4, :], z[:, 3, :], EPS_GATE, None, ALU.add))
                    link(12, nc.vector.reciprocal(z[:, 5, :], z[:, 4, :]))
                    link(13, nc.vector.tensor_tensor(gate[par][:, :, :], sel[:, :, :], wide(z_(5)), ALU.mult))
                if part == 6:
                    link(14, nc.vector.tensor_reduce(z[:, 0, :], gate[par][:, :, :], AX.X, ALU.add))
                    nc.vector.tensor_scalar(etop[par][:, :], z[:, 0, :], EPS_GATE, None, ALU.mult)
                    link(15, nc.vector.tensor_scalar(z[:, 1, :], z[:, 0, :], EPS_GATE, None, ALU.max))
                    dve.wait_ge(r_seq, nth(i, R_STEPS, 15))
                    link(16, nc.vector.reciprocal(z[:, 2, :], z[:, 1, :]))
                    dve.wait_ge(r_seq, nth(i, R_STEPS, 16))
                    nc.vector.tensor_tensor(gate[par][:, :, :], gate[par][:, :, :], wide(z_(2)), ALU.mult).then_inc(gates_ready, 1)

            def step(tag, i, par, first, front, attend):
                kind, k = tag
                mb = bank(tag, i, first, front) if kind in USES and (front if kind in IN_FRONT else attend) else None
                f = 0 if first else i + 1
                pf = 0 if first else 1 - par
                j, pj = i - 1, 1 - par
                use = use_no(tag, i, first, front) if kind in USES and (front if kind in IN_FRONT else attend) else None
                if front and kind == "LN1":
                    ln1(f, k)
                    if first and k == 2:
                        split_weights()
                if first and kind == "KVb":
                    for p in range(2):
                        nc.vector.memset(kst[p][ROWS:ROWS + MAXPARTS, :, :], 1.0)
                        nc.vector.memset(v3[p][:, :, 3 * HD:VW + 1], 1.0)
                if front and kind == "T":
                    dve.wait_ge(misc_full, use + 1)
                    dve.wait_ge(xT_high, nth(f, 3, k + 1))
                    if k < KC:
                        d, s, h = xT_l[:, k, 0:BLOCK], mb[:, :], xT_h[:, k, 0:BLOCK]
                    else:
                        d, h = xT_l[:, :, BLOCK:HALO], xT_h[:, :, BLOCK:HALO]
                        s = mb[:, 0:KC * 2 * HALF].rearrange("p (c n) -> p c n", c=KC)
                    nc.vector.tensor_tensor(d, s, h.bitcast(F32), ALU.subtract).then_inc(misc_free, 1)
                if front and kind == "Q":
                    dve.wait_ge(misc_full, use + 1)
                    dve.wait_ge(q1_done, nth(f, 2, k + 1))
                    if not first:
                        dve.wait_ge(k3_done, nth(f, 1, 1))
                        dve.wait_ge(v3_done, nth(f, 1, 1))
                    nc.vector.scalar_tensor_tensor(out=by_sub(rq[:, k, :]), in0=by_sub(mb[:, :]), scalar=bq_c[:, k:k + 1],
                                                   in1=qp[:, 0, :, k, :], op0=ALU.add, op1=ALU.subtract).then_inc(misc_free, 1)
                if front and kind == "KV":
                    h = HALO // 2
                    dve.wait_ge(misc_full, use + 1)
                    dve.wait_ge(k1_done, nth(f, 2, k + 1))
                    dve.wait_ge(q3_done, nth(f, 2, 2 if first else 0))
                    nc.vector.tensor_tensor(rk[:, k * h:(k + 1) * h], mb[0:32, 0:h], kp[:, 0, k * h:(k + 1) * h],
                                            ALU.subtract).then_inc(misc_free, 1)
                if front and kind == "VT":
                    dve.wait_ge(misc_full, use + 1)
                    dve.wait_ge(v1_done, nth(f, 1, 1))
                    nc.vector.tensor_tensor(rv[:, :, :], mb[:, 0:SUBS * 32].rearrange("p (c d) -> p c d", d=HD),
                                            v3[pf][:, :, 0:HD], ALU.subtract).then_inc(misc_free, 1)
                if attend and kind == "S":
                    dve.wait_ge(s_full, nth(i, SUBS, k + 1))
                    settled()
                    nc.vector.copy_predicated(s_ps[:, :, 0:SUB], upper[:, :, :], s_ps[:, :, SUB:2 * SUB]).then_inc(s_sel, 1)
                    dve.wait_ge(s_sel, nth(i, SUBS, k + 1))
                    nc.vector.tensor_reduce(negmax[:, k % 2, :], s_ps[:, :, 0:SUB], AX.X, ALU.max, negate=True).then_inc(max_done, 1)
                if attend and kind == "MT":
                    dve.wait_ge(misc_full, use + 1)
                    if not (isinstance(i, int) and i == 0 and k < 2):
                        dve.wait_ge(m_in[k % 2], nth(i, 32 * SUBS // 2, 32 * (k // 2)))
                    nc.vector.tensor_copy(mp[:, k % 2, 0, :], mb[0:PAIRS, 0:P]).then_inc(m1_done, 1)
                    dve.wait_ge(m1_done, nth(i, SUBS, k + 1))
                    nc.vector.tensor_tensor(mp[:, k % 2, 1, :], mb[0:PAIRS, 0:P], mp[:, k % 2, 0, :], ALU.subtract).then_inc(misc_free, 1)
                if attend and kind == "PV":
                    dve.wait_ge(misc_full, use + 1)
                    if not (isinstance(i, int) and i == 0 and k == 0):
                        dve.wait_ge(o_done, nth(i, SUBS, k))
                    part = mb[:, 0:PAIRS * VW].rearrange("p (a w) -> p a w", w=VW)
                    nc.vector.tensor_reduce(osum[:, :, :], part[:, :, 0:3 * HD].rearrange("p a (s d) -> p a d s", s=3),
                                            AX.X, ALU.add)
                    nc.vector.reciprocal(rden[:, :], part[:, :, 3 * HD]).then_inc(misc_free, 1)
                    dve.wait_ge(misc_free, use + 1)
                    nc.vector.tensor_tensor(o[:, k % 4, :].rearrange("p (a d) -> p a d", d=HD), osum[:, :, :],
                                            rden[:, :].rearrange("p (a d) -> p a d", d=1).broadcast_to([P, PAIRS, HD]), ALU.mult).then_inc(o_done, 1)
                if attend and kind == "OT":
                    dve.wait_ge(misc_full, use + 1)
                    dve.wait_ge(oT_high, nth(i, TILES, k + 1))
                    nc.vector.tensor_tensor(oT_l[:, :, :].rearrange("p r (s q) -> p s r q", s=2),
                                            mb[:, 0:2 * P].rearrange("p (s r q) -> p s r q", s=2, r=2),
                                            oT_h[:, :, :].bitcast(F32).rearrange("p r (s q) -> p s r q", s=2), ALU.subtract).then_inc(misc_free, 1)
                if attend and kind == "WO":
                    dve.wait_ge(misc_full, use + 1)
                    dve.wait_ge(xb_ready, nth(i, 1, 1))
                    nc.vector.tensor_tensor(x1[par][:, k, :], mb[:, 0:DIM], x1[par][:, k, :], ALU.add).then_inc(misc_free, 1)
                    dve.wait_ge(misc_free, use + 1)
                    nc.vector.bn_stats(st2[:, k % 2, :], x1[par][:, k, :]).then_inc(ln2_stat, 1)
                    dve.wait_ge(ln2_stat, nth(i, TILES, k + 1))
                    settled()
                    nc.vector.bn_aggr(mv2[:, k % 2, :], st2[:, k % 2, :]).then_inc(ln2_mv, 1)
                if attend and kind == "XN":
                    dve.wait_ge(ln2_rstd, nth(i, TILES, k + 1))
                    nc.vector.tensor_scalar(xn2[:, k % 2, :], x1[par][:, k, :], mv2[:, k % 2, 0:1], rstd2[:, k % 2:k % 2 + 1],
                                            ALU.subtract, ALU.mult).then_inc(xn2_ready, 1)
                if attend and kind == "X2T":
                    dve.wait_ge(misc_full, use + 1)
                    dve.wait_ge(x2_high, nth(i, TILES, k + 1))
                    nc.vector.tensor_tensor(x2_l[par][:, :, k * P:(k + 1) * P], mb[:, 0:KC * P].rearrange("p (c n) -> p c n", c=KC),
                                            x2_h[par][:, :, k * P:(k + 1) * P].bitcast(F32), ALU.subtract).then_inc(misc_free, 1)
                if attend and kind == "LT":
                    dve.wait_ge(misc_full, use + 1)
                    nc.vector.tensor_scalar(lT[:, :], mb[R0:R2, :], rb_c[R0:R2, 0:1], None, ALU.add).then_inc(misc_free, 1)
                if attend and kind == "LG":
                    dve.wait_ge(misc_full, use + 1)
                    nc.vector.tensor_reduce(lg[:, :, 0:EXPERTS], mb[:, 0:TILES * 2 * (R1 - R0)].rearrange("p (t a n) -> p t n a", t=TILES, a=2)[:, :, 0:EXPERTS, :],
                                            AX.X, ALU.add).then_inc(misc_free, 1)
                if attend and kind == "R":
                    router(i, par, k)
                if kind == "M":
                    t, g = k // EG, k % EG
                    if g in BY_DVE:
                        a = BY_DVE.index(g)
                        dve.wait_ge(e_full, nth(j, TILES * EG, k + 1))
                        if k == 0:
                            dve.wait_ge(gates_ready, nth(j, 1, 1))
                        for q in range(2):
                            scale = gate[pj][:, t, 2 * g + q:2 * g + q + 1]
                            src = e_ps[:, k % 2, q * DIM:(q + 1) * DIM]
                            dst = acc[:, t % 2, q, :]
                            done = 2 * (t * len(BY_DVE) + a) + q
                            if a == 0 and q == 0:
                                wait_some(dve, y_done, nth(j, TILES, t - 1))
                            if a > 0:
                                dve.wait_ge(acc_seq, nth(j, 2 * TILES * len(BY_DVE), done - 1))
                            if a == 0 and q == 1:
                                ins = nc.vector.tensor_scalar(dst, src, scale, None, ALU.mult)
                            else:
                                ins = nc.vector.scalar_tensor_tensor(out=dst, in0=src, scalar=scale, in1=dst if a else x1[pj][:, t, :],
                                                                     op0=ALU.mult, op1=ALU.add)
                            ins.then_inc(acc_seq, 1)
                if kind == "E" and k % 2 == 1:
                    ex = k // 2
                    dve.wait_ge(e_high, ex + 1)
                    nc.vector.tensor_tensor(we_l[:, :, ex, :], stage[:, ex % STAGES, :].rearrange("p (c n) -> p c n", c=KC),
                                            we_h[:, :, ex, :].bitcast(F32), ALU.subtract).then_inc(e_split, 1)

            program(dve, step)

        @block.tensor
        def _(pe):
            pe.wait_ge(masks_up, 6)
            pe.wait_ge(zeroed, 3)

            def three(dst, pairs, close=True, opened=False):
                n = 0
                for w_high_, w_low_, x_high_, x_low_ in pairs:
                    for w, x in ((w_high_, x_high_), (w_high_, x_low_), (w_low_, x_high_)):
                        last = nc.tensor.matmul(dst, w, x, start=(n == 0 and not opened), stop=(close and n == 3 * len(pairs) - 1))
                        n += 1
                return last

            def step(tag, i, par, first, front, attend):
                kind, k = tag
                mb = bank(tag, i, first, front) if kind in USES and (front if kind in IN_FRONT else attend) else None
                f = 0 if first else i + 1
                pf = 0 if first else 1 - par
                j, pj = i - 1, 1 - par
                if kind in USES and (front if kind in IN_FRONT else attend):
                    use = use_no(tag, i, first, front)
                    if kind == "T" and k == 0:
                        pe.wait_ge(xn_ready, nth(f, 1, 1))
                    if kind == "MT":
                        pe.wait_ge(max_done, nth(i, SUBS, k + 1))
                    if kind == "OT":
                        pe.wait_ge(o_done, nth(i, SUBS, 2 * k + 2))
                    if kind == "X2T":
                        pe.wait_ge(xn2_ready, nth(i, TILES, k + 1))
                    needs = {"Q": ("T", KC), "KV": ("T", KC), "LT": ("X2T", TILES - 1), "LG": ("LT", 0), "WO": ("OT", k)}.get(kind)
                    c = i if isinstance(i, int) else 1
                    next_to = needs and use_no(tag, c, first, front) == use_no(needs, c, first, front) + 1
                    if next_to:
                        pe.wait_ge(misc_free, use)
                    elif not (isinstance(use, int) and use < 2):
                        pe.wait_ge(misc_free, use - 1)
                    if kind == "VT":
                        pe.wait_ge(k1_done, nth(f, 2, 2))
                    if tag in (("T", KC), ("VT", 0), ("LG", 0)):
                        pe.sem_inc(passed_pe, 1)
                if first and tag == ("Q", 0):
                    pe.wait_ge(w_split, 4)
                    pe.wait_ge(b_high, 2)
                if front and kind == "T":
                    if k < KC:
                        for n in range(TILES):
                            last = nc.tensor.transpose(mb[:, n * P:(n + 1) * P], xn[:, n, k * P:(k + 1) * P], ident[:, :])
                    else:
                        w = 2 * HALF
                        for c in range(KC):
                            last = nc.tensor.transpose(mb[:, c * w:(c + 1) * w], xn[0:w, TILES, c * P:(c + 1) * P], ident[0:w, 0:w])
                    last.then_inc(misc_full, 1)
                if front and kind == "Q":
                    three(mb[:, :], [(wq_h[:, c, k * P:(k + 1) * P], wq_l[:, c, k * P:(k + 1) * P],
                                        xT_h[:, c, HALF:HALF + BLOCK], xT_l[:, c, HALF:HALF + BLOCK]) for c in range(KC)]).then_inc(misc_full, 1)
                if front and kind == "KV":
                    h = HALO // 2
                    cols = slice(k * h, (k + 1) * h)
                    three(mb[:, 0:h], [(wkv_h[:, c, :], wkv_l[:, c, :], xT_h[:, c, cols], xT_l[:, c, cols]) for c in range(KC)], close=False)
                    nc.tensor.matmul(mb[:, 0:h], bkv_h[:, :], valid[:, pf * HALF + k * h:pf * HALF + (k + 1) * h], start=False, stop=False)
                    nc.tensor.matmul(mb[:, 0:h], bkv_l[:, :], valid[:, pf * HALF + k * h:pf * HALF + (k + 1) * h], start=False, stop=True).then_inc(misc_full, 1)
                if front and kind == "VT":
                    for c in range(SUBS):
                        last = nc.tensor.transpose(mb[:, c * 32:(c + 1) * 32], vT[32:64, c * SUB:c * SUB + P], ident[32:64, 32:64])
                    last.then_inc(misc_full, 1)
                if attend and kind == "S":
                    if k == 0:
                        pe.wait_ge(qk_in, nth(i, QK_LOADS, QK_LOADS))
                    if not (isinstance(i, int) and i == 0 and k == 0):
                        pe.wait_ge(max_done, nth(i, SUBS, k))
                    for a in range(PAIRS):
                        last = nc.tensor.matmul(s_ps[:, a, :], qst[par][0:ROWS, k, a * P:(a + 1) * P],
                                                kst[par][0:ROWS, a // (PAIRS // 2), k * SUB:k * SUB + P], start=True, stop=True)
                    last.then_inc(s_full, 1)
                if attend and kind == "MT":
                    nc.tensor.transpose(mb[0:PAIRS, 0:P], negmax[:, k % 2, :], ident[:, :]).then_inc(misc_full, 1)
                if attend and kind == "ST":
                    pe.wait_ge(m_in[k % 2], nth(i, 32 * SUBS // 2, 32 * (k // 2 + 1)))
                    if not (isinstance(i, int) and i == 0 and k == 0):
                        pe.wait_ge(exp_done, nth(i, SUBS, k))
                    for g in range(GROUPS):
                        nc.tensor.matmul(st_ps[:, g, :], kst[par][:, g, k * SUB:k * SUB + P],
                                         qst[par][:, k, g * 512:(g + 1) * 512], start=True, stop=False)
                        last = nc.tensor.matmul(st_ps[:, g, :], ident_b[:, :], far[:, :, :].rearrange("p h q -> p (h q)"), start=False, stop=True)
                    last.then_inc(st_full, 1)
                if attend and kind == "PV":
                    if k == 0:
                        pe.wait_ge(v3_done, nth(i, 1, 1))
                    pe.wait_ge(pl_done, nth(i, SUBS, k + 1))
                    for a in range(PAIRS):
                        v = v3[par][:, 2 * k + a // (PAIRS // 2), 0:VW]
                        nc.tensor.matmul(mb[:, a * VW:(a + 1) * VW], prob_h[:, a * P:(a + 1) * P], v, start=True, stop=False)
                        last = nc.tensor.matmul(mb[:, a * VW:(a + 1) * VW], prob_l[:, a * P:(a + 1) * P], v, start=False, stop=True)
                    last.then_inc(misc_full, 1)
                if attend and kind == "OT":
                    for s in range(2):
                        last = nc.tensor.transpose(mb[:, s * P:(s + 1) * P], o[:, (2 * k + s) % 4, :], ident[:, :])
                    last.then_inc(misc_full, 1)
                if attend and kind == "WO":
                    three(mb[:, 0:DIM], [(oT_h[:, r, :], oT_l[:, r, :], wo_h[:, r, :], wo_l[:, r, :]) for r in range(2)]).then_inc(misc_full, 1)
                if attend and kind == "X2T":
                    for c in range(KC):
                        last = nc.tensor.transpose(mb[:, c * P:(c + 1) * P], xn2[:, k % 2, c * P:(c + 1) * P], ident[:, :])
                    last.then_inc(misc_full, 1)
                if attend and kind == "LT":
                    n = 0
                    for c in range(KC):
                        for x in (x2_h, x2_l):
                            last = nc.tensor.matmul(mb[:, :], wkv_h[:, c, :], x[par][:, c, :], start=(n == 0), stop=(n == 2 * KC - 1))
                            n += 1
                    last.then_inc(misc_full, 1)
                if attend and kind == "LG":
                    w = 2 * (R1 - R0)
                    for t in range(TILES):
                        last = nc.tensor.transpose(mb[:, t * w:t * w + R2 - R0], lT[:, t * P:(t + 1) * P], ident[R0:R2, R0:R2])
                    last.then_inc(misc_full, 1)
                if kind == "M":
                    t, g = k // EG, k % EG
                    if k == 0 and isinstance(j, int) and j == 0:
                        pe.wait_ge(e_split, EXPERTS)
                    before = k - 2
                    if before >= 0 or not (isinstance(j, int) and j == 0):
                        tb, gb = before // EG, before % EG
                        if gb in BY_ACT:
                            pe.wait_ge(e_read_act, nth(j, TILES * len(BY_ACT), tb * len(BY_ACT) + BY_ACT.index(gb) + 1))
                        else:
                            pe.wait_ge(acc_seq, nth(j, 2 * TILES * len(BY_DVE), 2 * (tb * len(BY_DVE) + BY_DVE.index(gb) + 1)))
                    rows = slice(t * P, (t + 1) * P)
                    three(e_ps[:, k % 2, :], [(x2_h[pj][:, c, rows], x2_l[pj][:, c, rows], we_h[:, c, 2 * g:2 * g + 2, :], we_l[:, c, 2 * g:2 * g + 2, :])
                                              for c in range(KC)]).then_inc(e_full, 1)

            program(pe, step, LAGGING)




def kernel(L0_attn_x, L0_attn_Wq, L0_attn_bq, L0_attn_Wk, L0_attn_bk, L0_attn_Wv, L0_attn_bv, L0_attn_Wo, L0_attn_bo,
           L0_ffn_router_w, L0_ffn_router_b, L0_ffn_expert_w):
    import numpy as np
    import concourse.bacc as bacc
    from concourse.bass_utils import run_bass_kernel_spmd

    x = np.pad(np.asarray(L0_attn_x), ((0, 0), (HALF, HALF), (0, 0)))
    blocks = [x[b, s:s + HALO] for b in range(BATCH) for s in range(0, SEQ, BLOCK)]
    x_halo = np.stack(blocks + [np.zeros_like(blocks[0])])
    by_dim = (GROUPS, PER_GROUP, HD)
    wq = np.asarray(L0_attn_Wq).reshape(DIM, *by_dim).transpose(0, 1, 3, 2).reshape(DIM, DIM)
    bq = np.asarray(L0_attn_bq).reshape(by_dim).transpose(0, 2, 1).reshape(DIM)
    wk = np.asarray(L0_attn_Wk).reshape(DIM, GROUPS, HD).transpose(0, 2, 1).reshape(DIM, GROUPS * HD)
    bk = np.asarray(L0_attn_bk).reshape(GROUPS, HD).T.reshape(GROUPS * HD)
    wo = np.asarray(L0_attn_Wo).reshape(PAIRS, 2, HD, DIM).transpose(1, 0, 2, 3).reshape(DIM, DIM)
    arrays = {
        "x_halo": x_halo, "wq": wq, "bq": bq, "wk": wk, "bk": bk, "wv": L0_attn_Wv,
        "bv": L0_attn_bv, "wo": wo, "bo": L0_attn_bo, "rwt": np.asarray(L0_ffn_router_w).T,
        "rb": L0_ffn_router_b, "ew": L0_ffn_expert_w,
    }
    arrays = {k: np.ascontiguousarray(v) for k, v in arrays.items()}
    nc = bacc.Bacc("TRN2", target_bir_lowering=False, num_devices=1)
    args = [nc.dram_tensor(k, v.shape, mybir.dt.from_np(v.dtype), kind="ExternalInput").ap() for k, v in arrays.items()]
    out = nc.dram_tensor("out", (BLOCKS, BLOCK, DIM), F32, kind="ExternalOutput").ap()
    build(nc, *args, out)
    r = run_bass_kernel_spmd(nc, [arrays], core_ids=[0])
    return r.results[0]["out"].reshape(BATCH, SEQ, DIM)
```
